# Optimizing a Trainium2 kernel written in Bass

```python
import numpy as np
import jax
import jax.numpy as jnp

def _softmax(x, axis=-1):
    return jax.nn.softmax(x, axis=axis)

def _gelu(x):
    return jax.nn.gelu(x, approximate=True)

def _silu(x):
    return jax.nn.silu(x)

def _sigmoid(x):
    return jax.nn.sigmoid(x)

def _layernorm(x, axis=-1, eps=1e-05):
    m = jnp.mean(x, axis=axis, keepdims=True)
    v = jnp.var(x, axis=axis, keepdims=True)
    return (x - m) / jnp.sqrt(v + eps)

def _scatter_add(tgt, idx, src, axis=0):
    return tgt.at[idx].add(src)

def _segment_sum(src, seg, n):
    return jax.ops.segment_sum(src, seg, n)
kernel_name = 'mk_xattn_seq_d4_seqx_r8_29b445'

def setup_inputs(seed: int=0):
    np.random.seed(seed)
    _w = jnp.asarray

    def _rec_inputs():
        import jax
        import jax.numpy as jnp
        _rk = jax.random.key(seed)
        x = 0.0003765 + 1 * jax.random.normal(jax.random.fold_in(_rk, 1), (64, 128, 128), jnp.float32)
        _lenS = 128 - jax.random.randint(jax.random.fold_in(_rk, 7), (64,), 0, max(1, 128 // 4) + 1, jnp.int32)
        _lenS2 = 77 - jax.random.randint(jax.random.fold_in(_rk, 8), (64,), 0, max(1, 77 // 4) + 1, jnp.int32)
        _ctx_1024P = jax.random.normal(jax.random.fold_in(_rk, 11), (64, 16, 128), jnp.float32)
        _ctx_1024c = jax.random.dirichlet(jax.random.fold_in(_rk, 511), 0.3 * jnp.ones((16,), jnp.float32), (64, 77))
        _ctx_1024t = jnp.einsum('bsk,bkd->bsd', _ctx_1024c, _ctx_1024P)
        _ctx_1024t = _ctx_1024t * jax.lax.rsqrt(jnp.mean(jnp.square(_ctx_1024t)) + 1e-12) * 0.953939
        ctx_1024 = -0.000292821 + 1.00034 * (_ctx_1024t + 0.3 * jax.random.normal(jax.random.fold_in(_rk, 611), (64, 77, 128), jnp.float32))
        _validS = jnp.arange(128)[None, :] < _lenS[:, None]
        _validS2 = jnp.arange(77)[None, :] < _lenS2[:, None]
        _causal = jnp.tril(jnp.ones((128, 128), dtype=bool))
        mask_Bx1x1xS2_if1 = jnp.where(jnp.ones((64, 1, 1, 77), dtype=bool), 1, 0).astype(jnp.int32)
        mask_Bx1xSxS2_ff0 = jnp.where(jnp.ones((64, 1, 128, 77), dtype=bool), 0.0, -1000000000.0).astype(jnp.float32)
        return (x, ctx_1024, mask_Bx1x1xS2_if1, mask_Bx1xSxS2_ff0)
    x, ctx_1024, mask_Bx1x1xS2_if1, mask_Bx1xSxS2_ff0 = _rec_inputs()

    def _L0_xattn_setup():
        import jax, jax.numpy as jnp
        import numpy as np
        EMBED = 128
        HEADS = 16
        HEAD_DIM = EMBED // HEADS
        FF = 4 * EMBED
        EPS = 1e-05

        def layernorm(x, g, b):
            mu = jnp.mean(x, axis=-1, keepdims=True)
            var = jnp.mean((x - mu) ** 2, axis=-1, keepdims=True)
            return (x - mu) * jax.lax.rsqrt(var + EPS) * g + b
        key = jax.random.key(seed)
        ks = jax.random.split(key, 16)
        B, S = (2, 256)
        f32 = jnp.float32
        inp = {'value': jax.random.normal(ks[0], (B, S, EMBED), f32), 'key': jax.random.normal(ks[1], (B, S, EMBED), f32), 'query': jax.random.normal(ks[2], (B, S, EMBED), f32), 'mask': jnp.ones((B, 1, 1, S), jnp.int32), 'wv': jax.random.normal(ks[3], (HEAD_DIM, HEAD_DIM), f32) * 0.02, 'wk': jax.random.normal(ks[4], (HEAD_DIM, HEAD_DIM), f32) * 0.02, 'wq': jax.random.normal(ks[5], (HEAD_DIM, HEAD_DIM), f32) * 0.02, 'w_out': jax.random.normal(ks[6], (EMBED, EMBED), f32) * 0.02, 'b_out': jnp.zeros((EMBED,), f32), 'g1': jnp.ones((EMBED,), f32), 'beta1': jnp.zeros((EMBED,), f32), 'w_ff1': jax.random.normal(ks[7], (EMBED, FF), f32) * 0.02, 'b_ff1': jnp.zeros((FF,), f32), 'w_ff2': jax.random.normal(ks[8], (FF, EMBED), f32) * 0.02, 'b_ff2': jnp.zeros((EMBED,), f32), 'g2': jnp.ones((EMBED,), f32), 'beta2': jnp.zeros((EMBED,), f32)}
        return inp
    _L0_xattn_all = _L0_xattn_setup()
    _L0_xattn_in = {k: v for k, v in _L0_xattn_all.items() if k in ('wv', 'wk', 'wq', 'w_out', 'b_out', 'g1', 'beta1', 'w_ff1', 'b_ff1', 'w_ff2', 'b_ff2', 'g2', 'beta2')}
    del _L0_xattn_all

    def _L1_xattn_setup():
        import jax, jax.numpy as jnp
        import numpy as np
        B, LX, LY = (2, 256, 256)
        E, H = (128, 16)
        HD = E // H
        FF = 512
        EPS = 1e-05

        def _rope_tables(L, d):
            inv = 1.0 / 10000.0 ** (jnp.arange(0, d, 2, dtype=jnp.float32) / d)
            t = jnp.arange(L, dtype=jnp.float32)
            f = jnp.outer(t, inv)
            return (jnp.cos(f), jnp.sin(f))

        def _apply_rope(x, cos, sin):
            d2 = x.shape[-1] // 2
            x1, x2 = (x[..., :d2], x[..., d2:])
            c = cos[None, :, None, :]
            s = sin[None, :, None, :]
            return jnp.concatenate([x1 * c - x2 * s, x2 * c + x1 * s], axis=-1)

        def _ln(x, g, b):
            m = jnp.mean(x, axis=-1, keepdims=True)
            v = jnp.var(x, axis=-1, keepdims=True)
            return (x - m) / jnp.sqrt(v + EPS) * g + b

        def _attn(q, k, v, causal):
            s = jnp.einsum('blhd,bmhd->bhlm', q, k)
            if causal:
                Lq, Lk = (s.shape[2], s.shape[3])
                mask = jnp.tril(jnp.ones((Lq, Lk), dtype=bool))
                s = jnp.where(mask, s, -jnp.inf)
            p = jax.nn.softmax(s, axis=-1)
            return jnp.einsum('bhlm,bmhd->blhd', p, v)

        def _forward(x, y, ln1_g, ln1_b, sa_wq, sa_bq, sa_wk, sa_bk, sa_wv, sa_bv, sa_wo, sa_bo, ln2_g, ln2_b, ca_wq, ca_bq, ca_wk, ca_bk, ca_wv, ca_bv, ca_wo, ca_bo, ln3_g, ln3_b, fc1_w, fc1_b, fc2_w, fc2_b):
            Bx, Lx, _ = x.shape
            Ly = y.shape[1]
            cos, sin = _rope_tables(max(Lx, Ly), HD)
            scale = HD ** (-0.5)
            h = _ln(x, ln1_g, ln1_b)
            q = (h @ sa_wq + sa_bq).reshape(Bx, Lx, H, HD) * scale
            k = (h @ sa_wk + sa_bk).reshape(Bx, Lx, H, HD)
            v = (h @ sa_wv + sa_bv).reshape(Bx, Lx, H, HD)
            q = _apply_rope(q, cos[:Lx], sin[:Lx])
            k = _apply_rope(k, cos[:Lx], sin[:Lx])
            a = _attn(q, k, v, causal=True).reshape(Bx, Lx, E)
            x = x + (a @ sa_wo + sa_bo)
            h = _ln(x, ln2_g, ln2_b)
            q = (h @ ca_wq + ca_bq).reshape(Bx, Lx, H, HD) * scale
            k = (y @ ca_wk + ca_bk).reshape(Bx, Ly, H, HD)
            v = (y @ ca_wv + ca_bv).reshape(Bx, Ly, H, HD)
            q = _apply_rope(q, cos[:Lx], sin[:Lx])
            k = _apply_rope(k, cos[:Ly], sin[:Ly])
            a = _attn(q, k, v, causal=False).reshape(Bx, Lx, E)
            x = x + (a @ ca_wo + ca_bo)
            h = _ln(x, ln3_g, ln3_b)
            return x + (jax.nn.gelu(h @ fc1_w + fc1_b) @ fc2_w + fc2_b)
        key = jax.random.key(seed)
        ks = jax.random.split(key, 16)

        def w(k, *s):
            return jax.random.normal(k, s, jnp.float32) * 0.02
        z = lambda *s: jnp.zeros(s, jnp.float32)
        o = lambda *s: jnp.ones(s, jnp.float32)
        return {'x': jax.random.normal(ks[0], (B, LX, E), jnp.float32), 'y': jax.random.normal(ks[1], (B, LY, E), jnp.float32), 'ln1_g': o(E), 'ln1_b': z(E), 'sa_wq': w(ks[2], E, E), 'sa_bq': z(E), 'sa_wk': w(ks[3], E, E), 'sa_bk': z(E), 'sa_wv': w(ks[4], E, E), 'sa_bv': z(E), 'sa_wo': w(ks[5], E, E), 'sa_bo': z(E), 'ln2_g': o(E), 'ln2_b': z(E), 'ca_wq': w(ks[6], E, E), 'ca_bq': z(E), 'ca_wk': w(ks[7], E, E), 'ca_bk': z(E), 'ca_wv': w(ks[8], E, E), 'ca_bv': z(E), 'ca_wo': w(ks[9], E, E), 'ca_bo': z(E), 'ln3_g': o(E), 'ln3_b': z(E), 'fc1_w': w(ks[10], E, FF), 'fc1_b': z(FF), 'fc2_w': w(ks[11], FF, E), 'fc2_b': z(E)}
    _L1_xattn_all = _L1_xattn_setup()
    _L1_xattn_in = {k: v for k, v in _L1_xattn_all.items() if k in ('ln1_g', 'ln1_b', 'sa_wq', 'sa_bq', 'sa_wk', 'sa_bk', 'sa_wv', 'sa_bv', 'sa_wo', 'sa_bo', 'ln2_g', 'ln2_b', 'ca_wq', 'ca_bq', 'ca_wk', 'ca_bk', 'ca_wv', 'ca_bv', 'ca_wo', 'ca_bo', 'ln3_g', 'ln3_b', 'fc1_w', 'fc1_b', 'fc2_w', 'fc2_b')}
    del _L1_xattn_all

    def _L2_xattn_setup():
        import jax, jax.numpy as jnp
        import numpy as np
        import math
        H, NH, NKV, HD, FF = (128, 16, 4, 64, 512)
        B, S = (2, 256)
        EPS, THETA = (1e-06, 10000.0)

        def _rmsnorm(x, w, eps=EPS):
            v = jnp.mean(x.astype(jnp.float32) ** 2, axis=-1, keepdims=True)
            return (x.astype(jnp.float32) * jax.lax.rsqrt(v + eps)).astype(x.dtype) * w

        def _rope_tables(seq_len, head_dim, theta=THETA):
            inv_freq = 1.0 / theta ** (jnp.arange(0, head_dim, 2, dtype=jnp.float32) / head_dim)
            freqs = jnp.arange(seq_len, dtype=jnp.float32)[:, None] * inv_freq[None, :]
            emb = jnp.concatenate([freqs, freqs], axis=-1)
            return (jnp.cos(emb), jnp.sin(emb))

        def _rotate_half(x):
            x1, x2 = jnp.split(x, 2, axis=-1)
            return jnp.concatenate([-x2, x1], axis=-1)

        def _apply_rope(x, cos, sin):
            return x * cos[None, None] + _rotate_half(x) * sin[None, None]
        key = jax.random.key(seed)
        ks = jax.random.split(key, 12)
        std = 0.02
        return {'hidden_states': jax.random.normal(ks[0], (B, S, H), jnp.float32), 'kv_states': jax.random.normal(ks[1], (B, S, H), jnp.float32), 'attention_mask': jnp.zeros((B, 1, S, S), jnp.float32), 'ln1_w': jnp.ones((H,), jnp.float32), 'ln2_w': jnp.ones((H,), jnp.float32), 'Wq': jax.random.normal(ks[2], (H, NH * HD), jnp.float32) * std, 'Wk': jax.random.normal(ks[3], (H, NKV * HD), jnp.float32) * std, 'Wv': jax.random.normal(ks[4], (H, NKV * HD), jnp.float32) * std, 'Wo': jax.random.normal(ks[5], (NH * HD, H), jnp.float32) * std, 'Wgate': jax.random.normal(ks[6], (H, FF), jnp.float32) * std, 'Wup': jax.random.normal(ks[7], (H, FF), jnp.float32) * std, 'Wdown': jax.random.normal(ks[8], (FF, H), jnp.float32) * std}
    _L2_xattn_all = _L2_xattn_setup()
    _L2_xattn_in = {k: v for k, v in _L2_xattn_all.items() if k in ('ln1_w', 'ln2_w', 'Wq', 'Wk', 'Wv', 'Wo', 'Wgate', 'Wup', 'Wdown')}
    del _L2_xattn_all

    def _L3_xattn_setup():
        import jax, jax.numpy as jnp
        import numpy as np
        H = 16
        DH = 32
        SCALE = DH ** (-0.5)
        EPS = 1e-05

        def rope(x):
            d, n = (x.shape[-1], x.shape[-2])
            inv_freq = 1.0 / 10000.0 ** (jnp.arange(0, d, 2, dtype=jnp.float32) / d)
            freqs = jnp.arange(n, dtype=jnp.float32)[:, None] * inv_freq[None, :]
            freqs = jnp.repeat(freqs, 2, axis=-1)
            cos, sin = (jnp.cos(freqs), jnp.sin(freqs))
            x1, x2 = (x[..., ::2], x[..., 1::2])
            x_rot = jnp.stack([-x2, x1], axis=-1).reshape(x.shape)
            return x * cos + x_rot * sin

        def split_heads(x):
            b, n, _ = x.shape
            return x.reshape(b, n, H, DH).transpose(0, 2, 1, 3)

        def merge_heads(x):
            b, h, n, d = x.shape
            return x.transpose(0, 2, 1, 3).reshape(b, n, h * d)

        def attend(q, k, v):
            q = rope(q * SCALE)
            k = rope(k)
            sim = jnp.einsum('bhid,bhjd->bhij', q, k)
            attn = jax.nn.softmax(sim, axis=-1)
            return jnp.einsum('bhij,bhjd->bhid', attn, v)

        def layer_norm(x, g, b):
            mu = jnp.mean(x, axis=-1, keepdims=True)
            var = jnp.var(x, axis=-1, keepdims=True)
            return (x - mu) * jax.lax.rsqrt(var + EPS) * g + b
        key = jax.random.key(seed)
        ks = jax.random.split(key, 16)
        D, DFF, HID = (128, 512, H * DH)
        s = lambda k, *sh: jax.random.normal(k, sh, dtype=jnp.float32) * 0.02
        return {'tgt': jax.random.normal(ks[0], (2, 256, D), dtype=jnp.float32), 'memory': jax.random.normal(ks[1], (2, 256, D), dtype=jnp.float32), 'w_qkv': s(ks[2], D, 3 * HID), 'w_out1': s(ks[3], HID, D), 'w_q': s(ks[4], D, HID), 'w_k': s(ks[5], D, HID), 'w_v': s(ks[6], D, HID), 'w_out2': s(ks[7], HID, D), 'w_ff1': s(ks[8], D, DFF), 'b_ff1': jnp.zeros((DFF,), jnp.float32), 'w_ff2': s(ks[9], DFF, D), 'b_ff2': jnp.zeros((D,), jnp.float32), 'g1': jnp.ones((D,), jnp.float32), 'be1': jnp.zeros((D,), jnp.float32), 'g2': jnp.ones((D,), jnp.float32), 'be2': jnp.zeros((D,), jnp.float32), 'g3': jnp.ones((D,), jnp.float32), 'be3': jnp.zeros((D,), jnp.float32)}
    _L3_xattn_all = _L3_xattn_setup()
    _L3_xattn_in = {k: v for k, v in _L3_xattn_all.items() if k in ('w_qkv', 'w_out1', 'w_q', 'w_k', 'w_v', 'w_out2', 'w_ff1', 'b_ff1', 'w_ff2', 'b_ff2', 'g1', 'be1', 'g2', 'be2', 'g3', 'be3')}
    del _L3_xattn_all
    return {'x': x, 'ctx_1024': ctx_1024, 'mask_Bx1x1xS2_if1': mask_Bx1x1xS2_if1, 'mask_Bx1xSxS2_ff0': mask_Bx1xSxS2_ff0, 'L0_xattn_wv': _L0_xattn_in['wv'], 'L0_xattn_wk': _L0_xattn_in['wk'], 'L0_xattn_wq': _L0_xattn_in['wq'], 'L0_xattn_w_out': _L0_xattn_in['w_out'], 'L0_xattn_b_out': _L0_xattn_in['b_out'], 'L0_xattn_g1': _L0_xattn_in['g1'], 'L0_xattn_beta1': _L0_xattn_in['beta1'], 'L0_xattn_w_ff1': _L0_xattn_in['w_ff1'], 'L0_xattn_b_ff1': _L0_xattn_in['b_ff1'], 'L0_xattn_w_ff2': _L0_xattn_in['w_ff2'], 'L0_xattn_b_ff2': _L0_xattn_in['b_ff2'], 'L0_xattn_g2': _L0_xattn_in['g2'], 'L0_xattn_beta2': _L0_xattn_in['beta2'], 'L1_xattn_ln1_g': _L1_xattn_in['ln1_g'], 'L1_xattn_ln1_b': _L1_xattn_in['ln1_b'], 'L1_xattn_sa_wq': _L1_xattn_in['sa_wq'], 'L1_xattn_sa_bq': _L1_xattn_in['sa_bq'], 'L1_xattn_sa_wk': _L1_xattn_in['sa_wk'], 'L1_xattn_sa_bk': _L1_xattn_in['sa_bk'], 'L1_xattn_sa_wv': _L1_xattn_in['sa_wv'], 'L1_xattn_sa_bv': _L1_xattn_in['sa_bv'], 'L1_xattn_sa_wo': _L1_xattn_in['sa_wo'], 'L1_xattn_sa_bo': _L1_xattn_in['sa_bo'], 'L1_xattn_ln2_g': _L1_xattn_in['ln2_g'], 'L1_xattn_ln2_b': _L1_xattn_in['ln2_b'], 'L1_xattn_ca_wq': _L1_xattn_in['ca_wq'], 'L1_xattn_ca_bq': _L1_xattn_in['ca_bq'], 'L1_xattn_ca_wk': _L1_xattn_in['ca_wk'], 'L1_xattn_ca_bk': _L1_xattn_in['ca_bk'], 'L1_xattn_ca_wv': _L1_xattn_in['ca_wv'], 'L1_xattn_ca_bv': _L1_xattn_in['ca_bv'], 'L1_xattn_ca_wo': _L1_xattn_in['ca_wo'], 'L1_xattn_ca_bo': _L1_xattn_in['ca_bo'], 'L1_xattn_ln3_g': _L1_xattn_in['ln3_g'], 'L1_xattn_ln3_b': _L1_xattn_in['ln3_b'], 'L1_xattn_fc1_w': _L1_xattn_in['fc1_w'], 'L1_xattn_fc1_b': _L1_xattn_in['fc1_b'], 'L1_xattn_fc2_w': _L1_xattn_in['fc2_w'], 'L1_xattn_fc2_b': _L1_xattn_in['fc2_b'], 'L2_xattn_ln1_w': _L2_xattn_in['ln1_w'], 'L2_xattn_ln2_w': _L2_xattn_in['ln2_w'], 'L2_xattn_Wq': _L2_xattn_in['Wq'], 'L2_xattn_Wk': _L2_xattn_in['Wk'], 'L2_xattn_Wv': _L2_xattn_in['Wv'], 'L2_xattn_Wo': _L2_xattn_in['Wo'], 'L2_xattn_Wgate': _L2_xattn_in['Wgate'], 'L2_xattn_Wup': _L2_xattn_in['Wup'], 'L2_xattn_Wdown': _L2_xattn_in['Wdown'], 'L3_xattn_w_qkv': _L3_xattn_in['w_qkv'], 'L3_xattn_w_out1': _L3_xattn_in['w_out1'], 'L3_xattn_w_q': _L3_xattn_in['w_q'], 'L3_xattn_w_k': _L3_xattn_in['w_k'], 'L3_xattn_w_v': _L3_xattn_in['w_v'], 'L3_xattn_w_out2': _L3_xattn_in['w_out2'], 'L3_xattn_w_ff1': _L3_xattn_in['w_ff1'], 'L3_xattn_b_ff1': _L3_xattn_in['b_ff1'], 'L3_xattn_w_ff2': _L3_xattn_in['w_ff2'], 'L3_xattn_b_ff2': _L3_xattn_in['b_ff2'], 'L3_xattn_g1': _L3_xattn_in['g1'], 'L3_xattn_be1': _L3_xattn_in['be1'], 'L3_xattn_g2': _L3_xattn_in['g2'], 'L3_xattn_be2': _L3_xattn_in['be2'], 'L3_xattn_g3': _L3_xattn_in['g3'], 'L3_xattn_be3': _L3_xattn_in['be3']}

def reference(x, ctx_1024, mask_Bx1x1xS2_if1, mask_Bx1xSxS2_ff0, L0_xattn_wv, L0_xattn_wk, L0_xattn_wq, L0_xattn_w_out, L0_xattn_b_out, L0_xattn_g1, L0_xattn_beta1, L0_xattn_w_ff1, L0_xattn_b_ff1, L0_xattn_w_ff2, L0_xattn_b_ff2, L0_xattn_g2, L0_xattn_beta2, L1_xattn_ln1_g, L1_xattn_ln1_b, L1_xattn_sa_wq, L1_xattn_sa_bq, L1_xattn_sa_wk, L1_xattn_sa_bk, L1_xattn_sa_wv, L1_xattn_sa_bv, L1_xattn_sa_wo, L1_xattn_sa_bo, L1_xattn_ln2_g, L1_xattn_ln2_b, L1_xattn_ca_wq, L1_xattn_ca_bq, L1_xattn_ca_wk, L1_xattn_ca_bk, L1_xattn_ca_wv, L1_xattn_ca_bv, L1_xattn_ca_wo, L1_xattn_ca_bo, L1_xattn_ln3_g, L1_xattn_ln3_b, L1_xattn_fc1_w, L1_xattn_fc1_b, L1_xattn_fc2_w, L1_xattn_fc2_b, L2_xattn_ln1_w, L2_xattn_ln2_w, L2_xattn_Wq, L2_xattn_Wk, L2_xattn_Wv, L2_xattn_Wo, L2_xattn_Wgate, L2_xattn_Wup, L2_xattn_Wdown, L3_xattn_w_qkv, L3_xattn_w_out1, L3_xattn_w_q, L3_xattn_w_k, L3_xattn_w_v, L3_xattn_w_out2, L3_xattn_w_ff1, L3_xattn_b_ff1, L3_xattn_w_ff2, L3_xattn_b_ff2, L3_xattn_g1, L3_xattn_be1, L3_xattn_g2, L3_xattn_be2, L3_xattn_g3, L3_xattn_be3):
    import jax
    import jax.numpy as jnp

    def _L0_xattn_ref(value, key, query, mask, wv, wk, wq, w_out, b_out, g1, beta1, w_ff1, b_ff1, w_ff2, b_ff2, g2, beta2):
        import jax, jax.numpy as jnp
        import numpy as np
        EMBED = 128
        HEADS = 16
        HEAD_DIM = EMBED // HEADS
        FF = 4 * EMBED
        EPS = 1e-05

        def layernorm(x, g, b):
            mu = jnp.mean(x, axis=-1, keepdims=True)
            var = jnp.mean((x - mu) ** 2, axis=-1, keepdims=True)
            return (x - mu) * jax.lax.rsqrt(var + EPS) * g + b
        B, S, E = query.shape
        v = value.reshape(B, -1, HEADS, HEAD_DIM) @ wv
        k = key.reshape(B, -1, HEADS, HEAD_DIM) @ wk
        q = query.reshape(B, -1, HEADS, HEAD_DIM) @ wq
        scores = jnp.einsum('bqhd,bkhd->bhqk', q, k)
        scores = jnp.where(mask == 0, jnp.float32(-1e+20), scores)
        attn = jax.nn.softmax(scores / jnp.sqrt(jnp.float32(EMBED)), axis=-1)
        out = jnp.einsum('bhqk,bkhd->bqhd', attn, v).reshape(B, S, E)
        attention = out @ w_out + b_out
        x = layernorm(attention + query, g1, beta1)
        ff = jax.nn.relu(x @ w_ff1 + b_ff1) @ w_ff2 + b_ff2
        return layernorm(ff + x, g2, beta2)

    def _L1_xattn_ref(x, y, ln1_g, ln1_b, sa_wq, sa_bq, sa_wk, sa_bk, sa_wv, sa_bv, sa_wo, sa_bo, ln2_g, ln2_b, ca_wq, ca_bq, ca_wk, ca_bk, ca_wv, ca_bv, ca_wo, ca_bo, ln3_g, ln3_b, fc1_w, fc1_b, fc2_w, fc2_b):
        import jax, jax.numpy as jnp
        import numpy as np
        B, LX, LY = (2, 256, 256)
        E, H = (128, 16)
        HD = E // H
        FF = 512
        EPS = 1e-05

        def _rope_tables(L, d):
            inv = 1.0 / 10000.0 ** (jnp.arange(0, d, 2, dtype=jnp.float32) / d)
            t = jnp.arange(L, dtype=jnp.float32)
            f = jnp.outer(t, inv)
            return (jnp.cos(f), jnp.sin(f))

        def _apply_rope(x, cos, sin):
            d2 = x.shape[-1] // 2
            x1, x2 = (x[..., :d2], x[..., d2:])
            c = cos[None, :, None, :]
            s = sin[None, :, None, :]
            return jnp.concatenate([x1 * c - x2 * s, x2 * c + x1 * s], axis=-1)

        def _ln(x, g, b):
            m = jnp.mean(x, axis=-1, keepdims=True)
            v = jnp.var(x, axis=-1, keepdims=True)
            return (x - m) / jnp.sqrt(v + EPS) * g + b

        def _attn(q, k, v, causal):
            s = jnp.einsum('blhd,bmhd->bhlm', q, k)
            if causal:
                Lq, Lk = (s.shape[2], s.shape[3])
                mask = jnp.tril(jnp.ones((Lq, Lk), dtype=bool))
                s = jnp.where(mask, s, -jnp.inf)
            p = jax.nn.softmax(s, axis=-1)
            return jnp.einsum('bhlm,bmhd->blhd', p, v)

        def _forward(x, y, ln1_g, ln1_b, sa_wq, sa_bq, sa_wk, sa_bk, sa_wv, sa_bv, sa_wo, sa_bo, ln2_g, ln2_b, ca_wq, ca_bq, ca_wk, ca_bk, ca_wv, ca_bv, ca_wo, ca_bo, ln3_g, ln3_b, fc1_w, fc1_b, fc2_w, fc2_b):
            Bx, Lx, _ = x.shape
            Ly = y.shape[1]
            cos, sin = _rope_tables(max(Lx, Ly), HD)
            scale = HD ** (-0.5)
            h = _ln(x, ln1_g, ln1_b)
            q = (h @ sa_wq + sa_bq).reshape(Bx, Lx, H, HD) * scale
            k = (h @ sa_wk + sa_bk).reshape(Bx, Lx, H, HD)
            v = (h @ sa_wv + sa_bv).reshape(Bx, Lx, H, HD)
            q = _apply_rope(q, cos[:Lx], sin[:Lx])
            k = _apply_rope(k, cos[:Lx], sin[:Lx])
            a = _attn(q, k, v, causal=True).reshape(Bx, Lx, E)
            x = x + (a @ sa_wo + sa_bo)
            h = _ln(x, ln2_g, ln2_b)
            q = (h @ ca_wq + ca_bq).reshape(Bx, Lx, H, HD) * scale
            k = (y @ ca_wk + ca_bk).reshape(Bx, Ly, H, HD)
            v = (y @ ca_wv + ca_bv).reshape(Bx, Ly, H, HD)
            q = _apply_rope(q, cos[:Lx], sin[:Lx])
            k = _apply_rope(k, cos[:Ly], sin[:Ly])
            a = _attn(q, k, v, causal=False).reshape(Bx, Lx, E)
            x = x + (a @ ca_wo + ca_bo)
            h = _ln(x, ln3_g, ln3_b)
            return x + (jax.nn.gelu(h @ fc1_w + fc1_b) @ fc2_w + fc2_b)
        return _forward(x, y, ln1_g, ln1_b, sa_wq, sa_bq, sa_wk, sa_bk, sa_wv, sa_bv, sa_wo, sa_bo, ln2_g, ln2_b, ca_wq, ca_bq, ca_wk, ca_bk, ca_wv, ca_bv, ca_wo, ca_bo, ln3_g, ln3_b, fc1_w, fc1_b, fc2_w, fc2_b)

    def _L2_xattn_ref(hidden_states, kv_states, attention_mask, ln1_w, ln2_w, Wq, Wk, Wv, Wo, Wgate, Wup, Wdown):
        import jax, jax.numpy as jnp
        import numpy as np
        import math
        H, NH, NKV, HD, FF = (128, 16, 4, 64, 512)
        B, S = (2, 256)
        EPS, THETA = (1e-06, 10000.0)

        def _rmsnorm(x, w, eps=EPS):
            v = jnp.mean(x.astype(jnp.float32) ** 2, axis=-1, keepdims=True)
            return (x.astype(jnp.float32) * jax.lax.rsqrt(v + eps)).astype(x.dtype) * w

        def _rope_tables(seq_len, head_dim, theta=THETA):
            inv_freq = 1.0 / theta ** (jnp.arange(0, head_dim, 2, dtype=jnp.float32) / head_dim)
            freqs = jnp.arange(seq_len, dtype=jnp.float32)[:, None] * inv_freq[None, :]
            emb = jnp.concatenate([freqs, freqs], axis=-1)
            return (jnp.cos(emb), jnp.sin(emb))

        def _rotate_half(x):
            x1, x2 = jnp.split(x, 2, axis=-1)
            return jnp.concatenate([-x2, x1], axis=-1)

        def _apply_rope(x, cos, sin):
            return x * cos[None, None] + _rotate_half(x) * sin[None, None]
        bsz, q_len, _ = hidden_states.shape
        k_len = kv_states.shape[1]
        residual = hidden_states
        h = _rmsnorm(hidden_states, ln1_w)
        kv = _rmsnorm(kv_states, ln1_w)
        q = (h @ Wq).reshape(bsz, q_len, NH, HD).transpose(0, 2, 1, 3)
        k = (kv @ Wk).reshape(bsz, k_len, NKV, HD).transpose(0, 2, 1, 3)
        v = (kv @ Wv).reshape(bsz, k_len, NKV, HD).transpose(0, 2, 1, 3)
        cos_q, sin_q = _rope_tables(q_len, HD)
        cos_k, sin_k = _rope_tables(k_len, HD)
        q = _apply_rope(q, cos_q, sin_q)
        k = _apply_rope(k, cos_k, sin_k)
        groups = NH // NKV
        k = jnp.repeat(k, groups, axis=1)
        v = jnp.repeat(v, groups, axis=1)
        scores = jnp.einsum('bhqd,bhkd->bhqk', q, k) / math.sqrt(HD)
        scores = scores + attention_mask
        probs = jax.nn.softmax(scores.astype(jnp.float32), axis=-1).astype(q.dtype)
        attn = jnp.einsum('bhqk,bhkd->bhqd', probs, v)
        attn = attn.transpose(0, 2, 1, 3).reshape(bsz, q_len, NH * HD)
        attn = attn @ Wo
        hidden = residual + attn
        residual = hidden
        x = _rmsnorm(hidden, ln2_w)
        x = jax.nn.silu(x @ Wgate) * (x @ Wup) @ Wdown
        return residual + x

    def _L3_xattn_ref(tgt, memory, w_qkv, w_out1, w_q, w_k, w_v, w_out2, w_ff1, b_ff1, w_ff2, b_ff2, g1, be1, g2, be2, g3, be3):
        import jax, jax.numpy as jnp
        import numpy as np
        H = 16
        DH = 32
        SCALE = DH ** (-0.5)
        EPS = 1e-05

        def rope(x):
            d, n = (x.shape[-1], x.shape[-2])
            inv_freq = 1.0 / 10000.0 ** (jnp.arange(0, d, 2, dtype=jnp.float32) / d)
            freqs = jnp.arange(n, dtype=jnp.float32)[:, None] * inv_freq[None, :]
            freqs = jnp.repeat(freqs, 2, axis=-1)
            cos, sin = (jnp.cos(freqs), jnp.sin(freqs))
            x1, x2 = (x[..., ::2], x[..., 1::2])
            x_rot = jnp.stack([-x2, x1], axis=-1).reshape(x.shape)
            return x * cos + x_rot * sin

        def split_heads(x):
            b, n, _ = x.shape
            return x.reshape(b, n, H, DH).transpose(0, 2, 1, 3)

        def merge_heads(x):
            b, h, n, d = x.shape
            return x.transpose(0, 2, 1, 3).reshape(b, n, h * d)

        def attend(q, k, v):
            q = rope(q * SCALE)
            k = rope(k)
            sim = jnp.einsum('bhid,bhjd->bhij', q, k)
            attn = jax.nn.softmax(sim, axis=-1)
            return jnp.einsum('bhij,bhjd->bhid', attn, v)

        def layer_norm(x, g, b):
            mu = jnp.mean(x, axis=-1, keepdims=True)
            var = jnp.var(x, axis=-1, keepdims=True)
            return (x - mu) * jax.lax.rsqrt(var + EPS) * g + b
        qkv = tgt @ w_qkv
        q, k, v = jnp.split(qkv, 3, axis=-1)
        sa = merge_heads(attend(split_heads(q), split_heads(k), split_heads(v))) @ w_out1
        x = layer_norm(tgt + sa, g1, be1)
        q = split_heads(x @ w_q)
        k = split_heads(memory @ w_k)
        v = split_heads(memory @ w_v)
        ca = merge_heads(attend(q, k, v)) @ w_out2
        x = layer_norm(x + ca, g2, be2)
        ff = jax.nn.gelu(x @ w_ff1 + b_ff1) @ w_ff2 + b_ff2
        return layer_norm(x + ff, g3, be3)
    x = _L0_xattn_ref(ctx_1024, ctx_1024, x, mask_Bx1x1xS2_if1, L0_xattn_wv, L0_xattn_wk, L0_xattn_wq, L0_xattn_w_out, L0_xattn_b_out, L0_xattn_g1, L0_xattn_beta1, L0_xattn_w_ff1, L0_xattn_b_ff1, L0_xattn_w_ff2, L0_xattn_b_ff2, L0_xattn_g2, L0_xattn_beta2)
    x = _L1_xattn_ref(x, ctx_1024, L1_xattn_ln1_g, L1_xattn_ln1_b, L1_xattn_sa_wq, L1_xattn_sa_bq, L1_xattn_sa_wk, L1_xattn_sa_bk, L1_xattn_sa_wv, L1_xattn_sa_bv, L1_xattn_sa_wo, L1_xattn_sa_bo, L1_xattn_ln2_g, L1_xattn_ln2_b, L1_xattn_ca_wq, L1_xattn_ca_bq, L1_xattn_ca_wk, L1_xattn_ca_bk, L1_xattn_ca_wv, L1_xattn_ca_bv, L1_xattn_ca_wo, L1_xattn_ca_bo, L1_xattn_ln3_g, L1_xattn_ln3_b, L1_xattn_fc1_w, L1_xattn_fc1_b, L1_xattn_fc2_w, L1_xattn_fc2_b)
    x = _L2_xattn_ref(x, ctx_1024, mask_Bx1xSxS2_ff0, L2_xattn_ln1_w, L2_xattn_ln2_w, L2_xattn_Wq, L2_xattn_Wk, L2_xattn_Wv, L2_xattn_Wo, L2_xattn_Wgate, L2_xattn_Wup, L2_xattn_Wdown)
    x = _L3_xattn_ref(x, ctx_1024, L3_xattn_w_qkv, L3_xattn_w_out1, L3_xattn_w_q, L3_xattn_w_k, L3_xattn_w_v, L3_xattn_w_out2, L3_xattn_w_ff1, L3_xattn_b_ff1, L3_xattn_w_ff2, L3_xattn_b_ff2, L3_xattn_g1, L3_xattn_be1, L3_xattn_g2, L3_xattn_be2, L3_xattn_g3, L3_xattn_be3)
    return x

_drawn_inputs = setup_inputs


def setup_inputs(seed=0):
    import zlib

    import numpy as np

    out = dict(_drawn_inputs(seed))
    spreads = {'L0_xattn_b_out': (0.0, 0.1),
     'L0_xattn_g1': (1.0, 0.2),
     'L0_xattn_beta1': (0.0, 0.1),
     'L0_xattn_b_ff1': (0.0, 0.272),
     'L0_xattn_b_ff2': (0.0, 0.1),
     'L0_xattn_g2': (1.0, 0.2),
     'L0_xattn_beta2': (0.0, 0.1),
     'L1_xattn_ln1_g': (1.0, 0.6),
     'L1_xattn_ln1_b': (0.0, 0.8),
     'L1_xattn_sa_bq': (0.0, 0.8),
     'L1_xattn_sa_bk': (0.0, 0.8),
     'L1_xattn_sa_bv': (0.0, 0.436),
     'L1_xattn_sa_bo': (0.0, 0.1),
     'L1_xattn_ln2_g': (1.0, 0.6),
     'L1_xattn_ln2_b': (0.0, 0.8),
     'L1_xattn_ca_bq': (0.0, 2.0),
     'L1_xattn_ca_bk': (0.0, 2.0),
     'L1_xattn_ca_bv': (0.0, 0.359),
     'L1_xattn_ca_bo': (0.0, 0.1),
     'L1_xattn_ln3_g': (1.0, 0.6),
     'L1_xattn_ln3_b': (0.0, 0.8),
     'L1_xattn_fc1_b': (0.0, 0.367),
     'L1_xattn_fc2_b': (0.0, 0.1),
     'L2_xattn_ln1_w': (1.0, 0.6),
     'L2_xattn_ln2_w': (1.0, 0.6),
     'L3_xattn_b_ff1': (0.0, 0.308),
     'L3_xattn_b_ff2': (0.0, 0.1),
     'L3_xattn_g1': (1.0, 0.2),
     'L3_xattn_be1': (0.0, 0.1),
     'L3_xattn_g2': (1.0, 0.2),
     'L3_xattn_be2': (0.0, 0.1),
     'L3_xattn_g3': (1.0, 0.2),
     'L3_xattn_be3': (0.0, 0.1)}
    factors = {'L0_xattn_wv': 7.369,
     'L0_xattn_wk': 25.95,
     'L0_xattn_wq': 24.703,
     'L0_xattn_w_out': 7.831,
     'L1_xattn_sa_wq': 8.0,
     'L1_xattn_sa_wk': 8.0,
     'L1_xattn_sa_wv': 4.106,
     'L1_xattn_ca_wq': 8.0,
     'L1_xattn_ca_wk': 8.0,
     'L2_xattn_Wq': 8.0,
     'L2_xattn_Wk': 8.0,
     'L2_xattn_Wgate': 4.983,
     'L2_xattn_Wup': 4.969,
     'L2_xattn_Wdown': 4.933,
     'L3_xattn_w_q': 8.0,
     'L3_xattn_w_k': 8.0}
    for name, (base, spread) in spreads.items():
        noise = np.random.default_rng([zlib.crc32(name.encode()), seed]).standard_normal(out[name].shape)
        drawn = base * np.exp(spread * noise) if base else spread * noise
        out[name] = jnp.asarray(drawn.astype(out[name].dtype))
    for name, factor in factors.items():
        out[name] = (out[name] * factor).astype(out[name].dtype)
    return out
```

```python
from contextlib import ExitStack

import concourse.bass as bass
import concourse.mybir as mybir

F32 = mybir.dt.float32
F32R = mybir.dt.float32r
I32 = mybir.dt.int32
ALU = mybir.AluOpType
ACT = mybir.ActivationFunctionType
AX = mybir.AxisListType

B, S, E, SK = 64, 128, 128, 77
NH, FF = 16, 512
SKE = SK + 1
NC = 2
ITERS = B // NC
NBANK = 4
PV_N = 128

SMALL, WIDE, GQA = "small", "wide", "gqa"
ATT = [
    dict(kind=SMALL, hd=8, nk=SK, scale=128 ** -0.5, bias=None),
    dict(kind=SMALL, hd=8, nk=S, scale=8 ** -0.5, bias="causal"),
    dict(kind=SMALL, hd=8, nk=SK, scale=8 ** -0.5, bias=None),
    dict(kind=GQA, hd=64, nk=SK, scale=0.125, bias="mask"),
    dict(kind=WIDE, hd=32, nk=S, scale=32 ** -0.5, bias=None),
    dict(kind=WIDE, hd=32, nk=SK, scale=32 ** -0.5, bias=None),
]


def head_of(kind, j, p):
    if kind == SMALL:
        return 4 * p + j
    if kind == GQA:
        return 2 * (4 * (j // 2) + p) + j % 2
    return 4 * j + p


PV_UNITS = {SMALL: 1, GQA: 4, WIDE: 2}


def bank_plan():
    plan = [("xc_T", "feat_ready", 1), ("cn_T", "feat_ready", 1)]

    def add(event, n, *names):
        plan.extend((name, event, n) for name in names)

    def attention(a):
        kind = ATT[a]["kind"]
        if kind == SMALL:
            add("qkv_read", 1, f"qkv{a}")
            add("padT_ready", 1, f"qT{a}_0", f"kT{a}_0")
        elif kind == GQA:
            add("raw_ready", 1, f"q{a}_0", f"q{a}_1")
            add("raw_ready", 2, f"kv{a}")
            add("padT_ready", 1, f"qT{a}_0", f"qT{a}_1", f"kT{a}_0")
        else:
            add("raw_ready", 1, f"q{a}_0", f"k{a}", f"v{a}")
            add("padT_ready", 1, *[f"{x}T{a}_{j}" for x in "qk" for j in range(4)])
        add("score_read", 1, *[f"s{a}_{j}" for j in range(4)])
        add("nmT_ready", 1, f"nm{a}")
        add("probs_ready", 1, *[f"sT{a}_{j}" for j in range(4)])
        add("ao_ready", 1, *[f"pv{a}_{u}" for u in range(PV_UNITS[kind])])
        add("aoT_ready", 1, *[f"oT{a}_{u}" for u in range(2 if kind == GQA else 1)])
        add("added", 1, f"y{a}")

    def mlp(n):
        add("feat_ready", 1, f"h_T{n}")
        if n == 2:
            add("act_hidden", 1, "gate2")
            add("hidden2_ready", 1, "up2")
        else:
            add("act_hidden", 4, f"up{n}")
        add("added", 1, f"down{n}")

    attention(0)
    mlp(0)
    add("feat_ready", 1, "a_T1")
    attention(1)
    add("feat_ready", 1, "a_T2")
    attention(2)
    mlp(1)
    add("feat_ready", 1, "a_T3")
    attention(3)
    mlp(2)
    add("feat_ready", 1, "a_T4")
    attention(4)
    add("feat_ready", 1, "a_T5")
    attention(5)
    mlp(3)
    return plan


PLAN = bank_plan()
NAMES = [name for name, _, _ in PLAN]
PLACE = {name: (n % NBANK, n // NBANK) for n, name in enumerate(NAMES)}
USES = [sum(1 for n in range(len(PLAN)) if n % NBANK == b) for b in range(NBANK)]
PER_ITER = {
    "stats_ready": 11, "rstd_ready": 11, "tok_ready": 10, "pads_ready": 6, "raw8_ready": 2,
    "rot_ready": 5, "nm_ready": 6, "inputs_used": 1, "out_ready": 1,
}
READ_AT = {}
for _name, _event, _n in PLAN:
    PER_ITER[_event] = PER_ITER.get(_event, 0) + _n
    READ_AT[_name] = (_event, PER_ITER[_event])


def before(name):
    b, k = PLACE[name]
    at = NBANK * (k - 1) + b if k else NBANK * (USES[b] - 1) + b
    return NAMES[at], k == 0


STREAM = {'apply': 8, 'small': 10, 'gqa': 20, 'wide': 16, 'max': 3, 'inputs': 8}
V_OF = (1, 2, 3, 4, 5)
DVE_STEPS = 186

COLS = ["L1_ln1_g", "L1_ln1_b", "L1_ln2_g", "L1_ln2_b", "L1_ln3_g", "L1_ln3_b", "L2_ln1_w", "L2_ln2_w"]
ROWS = (["L1_sa_bq", "L1_sa_bk", "L1_sa_bv", "L1_ca_bq", "L1_ca_bk", "L1_ca_bv",
         "L0_b_out", "L1_sa_bo", "L1_ca_bo", "L0_b_ff2", "L1_fc2_b", "L3_b_ff2",
         "L0_g1", "L0_beta1", "L0_g2", "L0_beta2",
         "L3_g1", "L3_be1", "L3_g2", "L3_be2", "L3_g3", "L3_be3"])
MLP_BIAS = ["L0_b_ff1", "L1_fc1_b", None, "L3_b_ff1"]
HOST = ["ident", "causal", "selector", "cos8", "sin8", "cos64", "sin64", "cos32", "sin32"]
HOST_W = {"ident": S, "causal": S, "selector": NH, "cos8": 8, "sin8": 8, "cos64": 64, "sin64": 64,
          "cos32": 32, "sin32": 32}
HOST_AT = {n: sum(HOST_W[m] for m in HOST[:i]) for i, n in enumerate(HOST)}
HOST_N = sum(HOST_W.values())


def build(nc, ins, consts, out):
    ctx = ExitStack()
    with ctx:
        def sb(name, shape, dt=F32):
            return ctx.enter_context(nc.sbuf_tensor(name, shape, dt))

        def sem(name):
            return ctx.enter_context(nc.semaphore(name))

        w_in = {n[:2] + n[8:] if n[0] == "L" else n: ap for n, ap in ins.items()}

        def blocks(name, rows):
            return w_in[name].rearrange("(m p) n -> p m n", p=128) if rows > 128 else w_in[name]

        W0 = sb("W0", [128, 3, 128])
        W0o = sb("W0o", [128, 1, 128])
        W1s = sb("W1s", [128, 3, 128])
        W1so = sb("W1so", [128, 1, 128])
        W1c = sb("W1c", [128, 3, 128])
        W1co = sb("W1co", [128, 1, 128])
        W2q = sb("W2q", [128, 1024])
        W2kv = sb("W2kv", [128, 512])
        W2o = sb("W2o", [128, 8, 128])
        W4 = sb("W4", [128, 1536])
        W4o = sb("W4o", [128, 4, 128])
        W5 = sb("W5", [128, 3, 512])
        W5o = sb("W5o", [128, 4, 128])
        Wup = [sb(f"Wup{n}", [128, FF]) for n in range(4)]
        Wgate = sb("Wgate", [128, FF])
        Wdown = [sb(f"Wdown{n}", [128, 4, 128]) for n in range(4)]
        Wo = [W0o, W1so, W1co, W2o, W4o, W5o]
        cols = sb("cols", [128, len(COLS)])
        mlp_bias = sb("mlp_bias", [128, 4, 4])
        rows = sb("rows", [128, len(ROWS), 128])
        host = sb("host", [128, HOST_N])
        ident_r = sb("ident_r", [128, S], F32R)
        causal_r = sb("causal_r", [128, S], F32R)
        sel_r = sb("sel_r", [128, NH], F32R)
        sel1_r = sb("sel1_r", [128, NH], F32R)
        wait_carrier = sb("wait_carrier", [128, 1])
        minus_half = sb("minus_half", [128, 1])
        ident = host[:, HOST_AT["ident"]:HOST_AT["ident"] + S]

        def row(name):
            return rows[:, ROWS.index(name), :]

        def col(name):
            i = COLS.index(name)
            return cols[:, i:i + 1]

        def table(name):
            return host[:, HOST_AT[name]:HOST_AT[name] + HOST_W[name]]

        class Ctx:
            pass

        cs = []
        for c in range(NC):
            t = Ctx()
            t.x_in = sb(f"x_in{c}", [128, E])
            t.c_in = sb(f"c_in{c}", [128, E])
            t.mask_in = sb(f"mask_in{c}", [128, SK])
            t.key_mask = sb(f"key_mask{c}", [128, 1], I32)
            t.x = sb(f"x{c}", [128, E])
            t.xn = sb(f"xn{c}", [128, E])
            t.cn = sb(f"cn{c}", [128, E])
            t.y = sb(f"y{c}", [128, E])
            t.stats = sb(f"stats{c}", [128, 6])
            t.mv = sb(f"mv{c}", [128, 2])
            t.var = sb(f"var{c}", [128, 1])
            t.rstd = sb(f"rstd{c}", [128, 1])
            t.xcT = sb(f"xcT{c}", [128, 2, 128])
            t.cnT = sb(f"cnT{c}", [128, 128])
            t.hT = sb(f"hT{c}", [128, 128])
            t.zero = sb(f"zero{c}", [128, 1])
            t.keep = sb(f"keep{c}", [128, 1])
            t.kbias = sb(f"kbias{c}", [128, 1])
            t.raw = sb(f"raw{c}", [128, 1280])
            t.q8 = sb(f"q8{c}", [128, NH, 4, 8])
            t.k8 = sb(f"k8{c}", [128, NH, 4, 8])
            t.pads = sb(f"pads{c}", [128, 2, NH, 3, 32])
            t.v8 = {nk: sb(f"v8_{nk}_{c}", [128, NH * 9 + PV_N]) for nk in (S, SK)}
            t.v32 = {nk: sb(f"v32_{nk}_{c}", [128, NH * 33 + PV_N]) for nk in (S, SK)}
            t.v64 = {SK: sb(f"v64_{c}", [128, 4 * 65 + PV_N])}
            t.qT = sb(f"qT{c}", [128, NH * S], F32R)
            t.kT = sb(f"kT{c}", [128, NH * S], F32R)
            t.qT64 = sb(f"qT64{c}", [128, 8 * S])
            t.kT64 = sb(f"kT64{c}", [128, 4 * S])
            t.nmax = sb(f"nmax{c}", [128, NH])
            t.nm = sb(f"nm{c}", [128, 4, 2, NH])
            t.nmT = sb(f"nmT{c}", [128, S], F32R)
            t.mask_hi = sb(f"mask_hi{c}", [128, SKE], F32R)
            t.mask_lo = sb(f"mask_lo{c}", [128, SKE], F32R)
            t.mask8 = sb(f"mask8{c}", [128, SKE])
            t.rsum = sb(f"rsum{c}", [128, NH])
            t.probs = t.pads[:, :, :, :, :].rearrange("p a h s d -> p (a h s d)")[:, 0:NH * S]
            t.turn = t.pads[:, :, :, :, :].rearrange("p a h s d -> p (a h s d)")[:, 0:1280]
            t.kdup = t.turn[:, 0:512]
            t.ao = t.raw[:, 0:1024]
            t.aoT = t.qT64[:, :]
            t.hid = t.kT64[:, :]
            t.gate = t.qT64[:, 0:512]
            cs.append(t)
        banks = [[ctx.enter_context(nc.psum_tensor(f"bank{c}_{b}", [128, 512], F32))
                  for b in range(NBANK)] for c in range(NC)]

        weights_in = sem("weights_in")
        consts_set = sem("consts_set")
        zeroed = sem("zeroed")
        dve_step = sem("dve_step")
        pool_step = sem("pool_step")
        loaded = [sem(f"loaded{c}") for c in range(NC)]
        stored = [sem(f"stored{c}") for c in range(NC)]
        full = [[sem(f"full{c}_{b}") for b in range(NBANK)] for c in range(NC)]
        stats_ready = [sem(f"stats_ready{c}") for c in range(NC)]
        rstd_ready = [sem(f"rstd_ready{c}") for c in range(NC)]
        tok_ready = [sem(f"tok_ready{c}") for c in range(NC)]
        feat_ready = [sem(f"feat_ready{c}") for c in range(NC)]
        pads_ready = [sem(f"pads_ready{c}") for c in range(NC)]
        qkv_read = [sem(f"qkv_read{c}") for c in range(NC)]
        raw8_ready = [sem(f"raw8_ready{c}") for c in range(NC)]
        raw_ready = [sem(f"raw_ready{c}") for c in range(NC)]
        rot_ready = [sem(f"rot_ready{c}") for c in range(NC)]
        padT_ready = [sem(f"padT_ready{c}") for c in range(NC)]
        score_read = [sem(f"score_read{c}") for c in range(NC)]
        nm_ready = [sem(f"nm_ready{c}") for c in range(NC)]
        nmT_ready = [sem(f"nmT_ready{c}") for c in range(NC)]
        probs_ready = [sem(f"probs_ready{c}") for c in range(NC)]
        ao_ready = [sem(f"ao_ready{c}") for c in range(NC)]
        aoT_ready = [sem(f"aoT_ready{c}") for c in range(NC)]
        added = [sem(f"added{c}") for c in range(NC)]
        act_hidden = [sem(f"act_hidden{c}") for c in range(NC)]
        hidden2_ready = [sem(f"hidden2_ready{c}") for c in range(NC)]
        inputs_used = [sem(f"inputs_used{c}") for c in range(NC)]
        out_ready = [sem(f"out_ready{c}") for c in range(NC)]
        ev = [dict(
            stats_ready=stats_ready[c],
            rstd_ready=rstd_ready[c],
            tok_ready=tok_ready[c],
            feat_ready=feat_ready[c],
            pads_ready=pads_ready[c],
            qkv_read=qkv_read[c],
            raw8_ready=raw8_ready[c],
            raw_ready=raw_ready[c],
            rot_ready=rot_ready[c],
            padT_ready=padT_ready[c],
            score_read=score_read[c],
            nm_ready=nm_ready[c],
            nmT_ready=nmT_ready[c],
            probs_ready=probs_ready[c],
            ao_ready=ao_ready[c],
            aoT_ready=aoT_ready[c],
            added=added[c],
            act_hidden=act_hidden[c],
            hidden2_ready=hidden2_ready[c],
            inputs_used=inputs_used[c],
            out_ready=out_ready[c],
        ) for c in range(NC)]

        def nth(it, name, n):
            return it * PER_ITER[name] + (PER_ITER[name] + n)

        def filled_count(it, name):
            b, k = PLACE[name]
            return it * USES[b] + (k + 1)

        def reader(c, name):
            return ev[c][READ_AT[name][0]]

        def read_count(it, name):
            return nth(it, *READ_AT[name])

        def last_reader(c, name):
            return reader(c, before(name)[0])

        def last_read_count(it, name):
            held, earlier = before(name)
            event, n = READ_AT[held]
            return nth(it, event, n - PER_ITER[event] if earlier else n)

        def v_tile(c, a):
            t, kind, nk = cs[c], ATT[a]["kind"], ATT[a]["nk"]
            return (t.v8 if kind == SMALL else t.v32 if kind == WIDE else t.v64)[nk]

        def v_heads(c, a):
            nk, hd = ATT[a]["nk"], ATT[a]["hd"]
            n = 4 if ATT[a]["kind"] == GQA else NH
            return v_tile(c, a)[0:nk, 0:n * (hd + 1)].rearrange("p (h d) -> p h d", h=n)

        def bank(c, name):
            return banks[c][PLACE[name][0]]

        def filled(c, name):
            return full[c][PLACE[name][0]]

        N_LOADS = 4
        vec_loads = []
        for i, (w, names) in enumerate([(W0o, ["L0_w_out"]), (W1so, ["L1_sa_wo"]), (W1co, ["L1_ca_wo"])]):
            vec_loads.append((w[:, 0, :], w_in[names[0]]))
        for w, names in ((W1s, ["L1_sa_wq", "L1_sa_wk", "L1_sa_wv"]), (W1c, ["L1_ca_wq", "L1_ca_wk", "L1_ca_wv"]),
                         (W5, ["L3_w_q", "L3_w_k", "L3_w_v"])):
            for i, n in enumerate(names):
                vec_loads.append((w[:, i, :], w_in[n]))
        vec_loads += [
            (W2q[:, :], w_in["L2_Wq"]), (W2kv[:, 0:256], w_in["L2_Wk"]), (W2kv[:, 256:512], w_in["L2_Wv"]),
            (W2o[:, :, :], blocks("L2_Wo", 1024)), (W4[:, :], w_in["L3_w_qkv"]),
            (W4o[:, :, :], blocks("L3_w_out1", 512)), (W5o[:, :, :], blocks("L3_w_out2", 512)),
            (Wup[0][:, :], w_in["L0_w_ff1"]), (Wup[1][:, :], w_in["L1_fc1_w"]),
            (Wup[2][:, :], w_in["L2_Wup"]), (Wup[3][:, :], w_in["L3_w_ff1"]), (Wgate[:, :], w_in["L2_Wgate"]),
            (Wdown[0][:, :, :], blocks("L0_w_ff2", 512)), (Wdown[1][:, :, :], blocks("L1_fc2_w", 512)),
            (Wdown[2][:, :, :], blocks("L2_Wdown", 512)), (Wdown[3][:, :, :], blocks("L3_w_ff2", 512)),
            (host[:, :], consts),
        ]
        for i, n in enumerate(COLS):
            vec_loads.append((cols[:, i:i + 1], w_in[n].rearrange("(p o) -> p o", o=1)))
        for i, n in enumerate(ROWS):
            vec_loads.append((rows[:, i, :], w_in[n].rearrange("(o n) -> o n", o=1).broadcast_to([128, 128])))
        for i, n in enumerate(MLP_BIAS):
            if n:
                vec_loads.append((mlp_bias[:, i, :], w_in[n].rearrange("(m p) -> p m", p=128)))
        N_DIAG = 3 * NH

        ctx.enter_context(nc.allow_non_contiguous_dma(reason="vectors, once, and the key mask"))
        block = ctx.enter_context(nc.Block())

        @block.sync
        def _(sp):
            for dst, src in vec_loads:
                sp.dma_start(dst, src).then_inc(weights_in, 16)
            sp.wait_ge(zeroed, 1 + NC)
            for i, n in enumerate(("L0_wq", "L0_wk", "L0_wv")):
                for h in range(NH):
                    sp.dma_start(W0[8 * h:8 * h + 8, i, 8 * h:8 * h + 8], w_in[n]).then_inc(weights_in, 16)

            def load(c, b):
                t = cs[c]
                sp.dma_start(t.x_in[:, :], w_in["x"][b]).then_inc(loaded[c], 16)
                sp.dma_start(t.c_in[0:SK, :], w_in["ctx_1024"][b]).then_inc(loaded[c], 16)
                sp.dma_start(t.mask_in[:, :], w_in["mask_Bx1xSxS2_ff0"][b, 0]).then_inc(loaded[c], 16)
                sp.dma_start(t.key_mask[0:SK, :],
                             w_in["mask_Bx1x1xS2_if1"][b, 0].rearrange("o k -> k o")).then_inc(loaded[c], 16)

            for c in range(NC):
                load(c, c)
            for c in range(NC):
                sp.sem_inc(stored[c], 16)
            with sp.Fori(0, ITERS - 1) as it:
                used = [sp.snap(it * PER_ITER["inputs_used"] + (PER_ITER["inputs_used"] + 1)) for c in range(NC)]
                ready = [sp.snap(it * PER_ITER["out_ready"] + (PER_ITER["out_ready"] + 1)) for c in range(NC)]
                for c in range(NC):
                    sp.wait_ge(inputs_used[c], used[c])
                    load(c, it * NC + (NC + c))
                for c in range(NC):
                    sp.wait_ge(out_ready[c], ready[c])
                    sp.dma_start(out[it * NC + c], cs[c].y[:, :]).then_inc(stored[c], 16)
            for c in range(NC):
                sp.wait_ge(out_ready[c], (ITERS + 1) * PER_ITER["out_ready"])
                sp.dma_start(out[(ITERS - 1) * NC + c], cs[c].y[:, :]).then_inc(stored[c], 16)
            for c in range(NC):
                sp.wait_ge(stored[c], 16 * (ITERS + 1))

        def stages():
            yield ("inputs",)
            yield from attention(0)
            yield ("norm", 1), ("normed", 1, "post", "L0_g1", "L0_beta1")
            yield from ()

        def attention(a):
            yield ("project", a)
            yield ("turn", a)
            yield ("stack", a)
            yield ("scores", a)
            yield ("max", a)
            yield ("probs", a)
            yield ("values", a)
            yield ("outT", a)
            yield ("out", a)

        def norm(n):
            yield ("stats", n)
            yield ("apply", n)

        def mlp(n):
            yield ("up", n)
            yield ("down", n)

        STAGES = [("inputs",)]
        for piece in (attention(0), norm(1), mlp(0), norm(2), norm(3), attention(1), norm(4), attention(2),
                      norm(5), mlp(1), norm(6), attention(3), norm(7), mlp(2), [("copyT",)], attention(4),
                      norm(8), attention(5), norm(9), mlp(3), norm(10)):
            STAGES.extend(piece)

        NORM = {0: ("rms", 1e-6, "L2_ln1_w", None), 1: ("post", 1e-5, "L0_g1", "L0_beta1"),
                2: ("post", 1e-5, "L0_g2", "L0_beta2"), 3: ("pre", 1e-5, "L1_ln1_g", "L1_ln1_b"),
                4: ("pre", 1e-5, "L1_ln2_g", "L1_ln2_b"), 5: ("pre", 1e-5, "L1_ln3_g", "L1_ln3_b"),
                6: ("rms", 1e-6, "L2_ln1_w", None), 7: ("rms", 1e-6, "L2_ln2_w", None),
                8: ("post", 1e-5, "L3_g1", "L3_be1"), 9: ("post", 1e-5, "L3_g2", "L3_be2"),
                10: ("post", 1e-5, "L3_g3", "L3_be3")}
        FEAT = ["xc_T", "cn_T", "h_T0", "a_T1", "a_T2", "h_T1", "a_T3", "h_T2", "a_T4", "a_T5", "h_T3"]
        FEAT_NORM = [None, 0, None, 3, 4, 5, 6, 7, None, None, None]
        NORM_FEAT = {0: 1, 1: 2, 3: 3, 4: 4, 5: 5, 6: 6, 7: 7, 8: 9, 9: 10}

        PROJECT_FEAT = [1, 4, 5, 7, 9, 10]
        UP_FEAT = [3, 6, 8, 11]
        PADT_UNITS = [2, 2, 2, 3, 8, 8]
        RAW_UNITS = [0, 0, 0, 4, 3, 3]
        AOT_UNITS = [1, 1, 1, 2, 1, 1]
        HID_UNITS = [4, 4, 1, 4]

        @block.tensor
        def _(pe):
            pe.wait_ge(weights_in, 16 * (len(vec_loads) + N_DIAG))
            pe.wait_ge(consts_set, 1)
            for c in range(NC):
                for name, n in PER_ITER.items():
                    pe.sem_inc(ev[c][name], n)
            with pe.Fori(0, ITERS) as it:
                order = [[], []]

                def stream(c, name, n):
                    for _ in range(n):
                        pe.matmul(bank(c, name)[:, :].rearrange("p (a n) -> p a n", a=4), ident_r[:, :],
                                  ident_r[:, :].unsqueeze(1).broadcast_to([128, 4, 128]), start=True, stop=True,
                                  skip_group_check=True)

                def transpose_into(c, name, pieces, taken=False):
                    if not taken:
                        take(c, name)
                    for i, src in enumerate(pieces):
                        last = pe.transpose(bank(c, name)[0:src.shape[1], 128 * i:128 * i + 128], src, ident)
                    last.then_inc(filled(c, name), 1)

                def product(c, name, pairs, at=0, last=True):
                    n = pairs[0][1].shape[-1]
                    for i, (lhsT, rhs) in enumerate(pairs):
                        mm = pe.matmul(bank(c, name)[:, at:at + n], lhsT, rhs,
                                       start=(i == 0), stop=(i == len(pairs) - 1))
                    if last:
                        mm.then_inc(filled(c, name), 1)

                def take(c, name):
                    pe.wait_ge(last_reader(c, name), last_read_count(it, name))
                    order[c].append(name)

                def to_features(c, f):
                    t = cs[c]
                    take(c, FEAT[f])
                    if c == 0 and f > 1:
                        stream(c, FEAT[f], STREAM["apply"])
                    pe.wait_ge(tok_ready[c], nth(it, "tok_ready", f))
                    src = {1: t.cn, 3: t.xn, 4: t.xn, 5: t.xn, 6: t.xn, 7: t.xn}.get(f, t.x)
                    transpose_into(c, FEAT[f], [src[:, :]], taken=True)

                def project(c, a):
                    t = cs[c]
                    pe.wait_ge(feat_ready[c], nth(it, "feat_ready", PROJECT_FEAT[a]))
                    hT = t.xcT[:, 0, :] if a == 0 else t.hT[:, :]
                    cT = t.xcT[:, 1, :]
                    if a in (0, 1, 2):
                        take(c, f"qkv{a}")
                        Wa = (W0, W1s, W1c)[a]
                        product(c, f"qkv{a}", [(hT, Wa[:, 0, :])], 0, False)
                        product(c, f"qkv{a}", [(hT if a == 1 else cT,
                                                Wa[:, 1:3, :].rearrange("p a n -> p (a n)"))], 128)
                    elif a == 3:
                        for u in range(2):
                            take(c, f"q3_{u}")
                            product(c, f"q3_{u}", [(hT, W2q[:, 512 * u:512 * u + 512])])
                        take(c, "kv3")
                        product(c, "kv3", [(t.cnT[:, :], W2kv[:, :])])
                    else:
                        for i, n in enumerate((f"q{a}_0", f"k{a}", f"v{a}")):
                            take(c, n)
                            if a == 4:
                                product(c, n, [(hT, W4[:, 512 * i:512 * i + 512])])
                            else:
                                product(c, n, [(cT if i else hT, W5[:, i, :])])

                def stack(c, a):
                    t = cs[c]
                    kind = ATT[a]["kind"]
                    first = f"qT{a}_0"
                    take(c, first)
                    if c == 0:
                        stream(c, first, STREAM[kind])
                    pe.wait_ge(pads_ready[c], nth(it, "pads_ready", a + 1))
                    if kind == SMALL:
                        for nm, src in ((f"qT{a}_0", t.q8), (f"kT{a}_0", t.k8)):
                            flat = src[:, :, :, :].rearrange("p h s d -> p (h s d)")
                            transpose_into(c, nm, [flat[:, 128 * i:128 * i + 128] for i in range(4)],
                                           taken=nm == first)
                    elif kind == GQA:
                        for u in range(2):
                            transpose_into(c, f"qT3_{u}",
                                           [t.raw[:, 512 * u + 128 * i:512 * u + 128 * i + 128] for i in range(4)],
                                           taken=u == 0)
                        transpose_into(c, "kT3_0", [t.kdup[:, 128 * i:128 * i + 128] for i in range(4)])
                    else:
                        for i, qk in enumerate("qk"):
                            for j in range(4):
                                transpose_into(c, f"{qk}T{a}_{j}",
                                               [t.pads[:, i, 4 * j + p, :, :].rearrange("p s d -> p (s d)")
                                                for p in range(4)], taken=i == 0 and j == 0)

                def operands(c, a, j, p):
                    t, kind = cs[c], ATT[a]["kind"]
                    h = head_of(kind, j, p)
                    if kind == SMALL:
                        rr = slice(32 * j, 32 * j + 32)
                        return t.qT[rr, 128 * p:128 * p + 128], t.kT[rr, 128 * p:128 * p + 128]
                    if kind == GQA:
                        rr = slice(64 * (h % 2), 64 * (h % 2) + 64)
                        q = 128 * (h // 2)
                        kv = 128 * (h // 4)
                        return t.qT64[rr, q:q + 128], t.kT64[rr, kv:kv + 128]
                    return t.qT[0:96, 128 * h:128 * h + 128], t.kT[0:96, 128 * h:128 * h + 128]

                def biases(c, a):
                    if ATT[a]["bias"] == "causal":
                        return [causal_r[:, :]]
                    if ATT[a]["bias"] == "mask":
                        return [cs[c].mask_hi[:, :], cs[c].mask_lo[:, :]]
                    return []

                def scores(c, a):
                    nk = ATT[a]["nk"]
                    nke = S if nk == S else SKE
                    pe.wait_ge(padT_ready[c], nth(it, "padT_ready", sum(PADT_UNITS[:a + 1])))
                    for j in range(4):
                        name = f"s{a}_{j}"
                        take(c, name)
                        dst = bank(c, name)[:, 0:4 * nke]
                        bs = biases(c, a)
                        for i, bias in enumerate(bs):
                            pe.matmul(dst.rearrange("q (h k) -> q h k", h=4), ident_r[:, :],
                                      bias.unsqueeze(1).broadcast_to([128, 4, nke]),
                                      start=(i == 0), stop=False, skip_group_check=True)
                        for p in range(4):
                            qT, kT = operands(c, a, j, p)
                            mm = pe.matmul(dst[:, nke * p:nke * p + nke], qT, kT[:, 0:nke],
                                           start=not bs, stop=True, skip_group_check=True)
                        mm.then_inc(filled(c, name), 1)

                def maxima(c, a):
                    take(c, f"nm{a}")
                    stream(c, f"nm{a}", STREAM["max"])
                    pe.wait_ge(nm_ready[c], nth(it, "nm_ready", a + 1))
                    transpose_into(c, f"nm{a}", [cs[c].nm[:, :, :, :].rearrange("p a b h -> p (a b h)")], taken=True)

                def scores_T(c, a):
                    t, nk, kind = cs[c], ATT[a]["nk"], ATT[a]["kind"]
                    pe.wait_ge(nmT_ready[c], nth(it, "nmT_ready", a + 1))
                    for j in range(4):
                        name = f"sT{a}_{j}"
                        take(c, name)
                        dst = bank(c, name)[0:nk, :]
                        bs = biases(c, a)
                        for i, bias in enumerate(bs):
                            pe.matmul(dst.rearrange("k (h q) -> k h q", h=4), bias[:, 0:nk],
                                      ident_r[:, :].unsqueeze(1).broadcast_to([128, 4, S]),
                                      start=(i == 0), stop=False, skip_group_check=True)
                        for p in range(4):
                            qT, kT = operands(c, a, j, p)
                            pe.matmul(dst[:, 128 * p:128 * p + 128], kT[:, 0:nk], qT,
                                      start=not bs, stop=False, skip_group_check=True)
                            rr = slice(32 * j, 32 * j + 32) if kind == SMALL else slice(0, 128)
                            sel = sel_r if kind == SMALL else sel1_r
                            mm = pe.matmul(dst[:, 128 * p:128 * p + 128],
                                           sel[rr, 4 * j + p:4 * j + p + 1].broadcast_to([rr.stop - rr.start, nk]),
                                           t.nmT[rr, :], start=False, stop=True, skip_group_check=True)
                        mm.then_inc(filled(c, name), 1)

                def values(c, a):
                    t, nk, kind, hd = cs[c], ATT[a]["nk"], ATT[a]["kind"], ATT[a]["hd"]
                    v = v_tile(c, a)
                    where = {head_of(kind, j, p): 4 * j + p for j in range(4) for p in range(4)}
                    pe.wait_ge(probs_ready[c], nth(it, "probs_ready", 4 * a + 4))
                    per = NH // PV_UNITS[kind]
                    for u in range(PV_UNITS[kind]):
                        name = f"pv{a}_{u}"
                        take(c, name)
                        for i in range(per):
                            h = u * per + i
                            at = 128 * where[h]
                            vh = (hd + 1) * (h // 4 if kind == GQA else h)
                            mm = pe.matmul(bank(c, name)[:, (hd + 1) * i:(hd + 1) * i + PV_N],
                                           t.probs[:, at:at + 128], v[:, vh:vh + PV_N],
                                           start=True, stop=True, skip_group_check=True)
                        mm.then_inc(filled(c, name), 1)

                def out_T(c, a):
                    n = NH * ATT[a]["hd"] // 128
                    pe.wait_ge(reader(c, f"pv{a}_{PV_UNITS[ATT[a]['kind']] - 1}"), read_count(it, f"pv{a}_{PV_UNITS[ATT[a]['kind']] - 1}"))
                    for u in range(AOT_UNITS[a]):
                        transpose_into(c, f"oT{a}_{u}", [cs[c].ao[:, 128 * i:128 * i + 128]
                                                         for i in range(4 * u, min(n, 4 * u + 4))])

                def out_product(c, a):
                    n = NH * ATT[a]["hd"] // 128
                    pe.wait_ge(aoT_ready[c], nth(it, "aoT_ready", sum(AOT_UNITS[:a + 1])))
                    take(c, f"y{a}")
                    product(c, f"y{a}", [(cs[c].aoT[:, 128 * i:128 * i + 128], Wo[a][:, i, :]) for i in range(n)])

                def up(c, n):
                    pe.wait_ge(feat_ready[c], nth(it, "feat_ready", UP_FEAT[n]))
                    for nm, W in ((f"up{n}", Wup[n]),) if n != 2 else (("gate2", Wgate), ("up2", Wup[2])):
                        take(c, nm)
                        for m in range(4):
                            product(c, nm, [(W[:, 128 * m:128 * m + 128], cs[c].hT[:, :])], 128 * m, m == 3)

                def down(c, n):
                    if n == 2:
                        pe.wait_ge(hidden2_ready[c], nth(it, "hidden2_ready", 1))
                    else:
                        pe.wait_ge(act_hidden[c], nth(it, "act_hidden", sum(HID_UNITS[:n + 1])))
                    take(c, f"down{n}")
                    product(c, f"down{n}", [(cs[c].hid[:, 128 * m:128 * m + 128], Wdown[n][:, m, :])
                                            for m in range(4)])

                for st in STAGES:
                    for c in range(NC):
                        if st[0] == "inputs":
                            w_loaded = it * (16 * N_LOADS) + 16 * N_LOADS
                            if c == 0:
                                take(c, "xc_T")
                                stream(c, "xc_T", STREAM["inputs"])
                            pe.wait_ge(loaded[c], w_loaded)
                            transpose_into(c, "xc_T", [cs[c].x_in[:, :], cs[c].c_in[:, :]], taken=c == 0)
                            to_features(c, 1)
                        elif st[0] == "project":
                            project(c, st[1])
                        elif st[0] == "stack":
                            stack(c, st[1])
                        elif st[0] == "scores":
                            scores(c, st[1])
                        elif st[0] == "max":
                            maxima(c, st[1])
                        elif st[0] == "probs":
                            scores_T(c, st[1])
                        elif st[0] == "values":
                            values(c, st[1])
                        elif st[0] == "outT":
                            out_T(c, st[1])
                        elif st[0] == "out":
                            out_product(c, st[1])
                        elif st[0] == "apply" and st[1] in NORM_FEAT:
                            to_features(c, NORM_FEAT[st[1]])
                        elif st[0] == "copyT":
                            to_features(c, 8)
                        elif st[0] == "up":
                            up(c, st[1])
                        elif st[0] == "down":
                            down(c, st[1])
                assert order[0] == NAMES and order[1] == NAMES, (order[0], NAMES)

        @block.scalar
        def _(act):
            act.wait_ge(weights_in, 16 * (len(vec_loads) + N_DIAG))
            with act.Fori(0, ITERS) as it:

                def evacuate(c, name, dst, width, event, scale=None, bias=None, n=128):
                    act.wait_ge(filled(c, name), filled_count(it, name))
                    act.activation(dst, bank(c, name)[0:n, 0:width], ACT.Identity,
                                   scale=1.0 if scale is None else scale,
                                   bias=0.0 if bias is None else bias).then_inc(event[c], 1)

                def to_features(c, f):
                    t = cs[c]
                    dst = t.xcT[:, :, :].rearrange("p a n -> p (a n)") if f == 0 else t.cnT[:, :] if f == 1 else t.hT[:, :]
                    g = b = None
                    if FEAT_NORM[f] is not None:
                        _, _, gain, shift = NORM[FEAT_NORM[f]]
                        g, b = col(gain), col(shift) if shift else None
                    evacuate(c, FEAT[f], dst, 256 if f == 0 else 128, feat_ready, g, b)

                def project(c, a):
                    t = cs[c]
                    if a == 3:
                        for u in range(2):
                            evacuate(c, f"q3_{u}", t.raw[:, 512 * u:512 * u + 512], 512, raw_ready)
                        act.wait_ge(filled(c, "kv3"), filled_count(it, "kv3"))
                        act.activation(t.raw[:, 1024:1280], bank(c, "kv3")[:, 0:256],
                                       ACT.Identity).then_inc(raw_ready[c], 1)
                        act.activation(v_heads(c, a)[:, :, 0:64],
                                       bank(c, "kv3")[0:SK, 256:512].rearrange("p (h d) -> p h d", h=4),
                                       ACT.Identity).then_inc(raw_ready[c], 1)
                    elif a > 3:
                        evacuate(c, f"q{a}_0", t.raw[:, 0:512], 512, raw_ready)
                        evacuate(c, f"k{a}", t.raw[:, 512:1024], 512, raw_ready)
                        act.wait_ge(filled(c, f"v{a}"), filled_count(it, f"v{a}"))
                        nk = ATT[a]["nk"]
                        act.activation(v_heads(c, a)[:, :, 0:32],
                                       bank(c, f"v{a}")[0:nk, :].rearrange("p (h d) -> p h d", h=NH),
                                       ACT.Identity).then_inc(raw_ready[c], 1)

                def stack(c, a):
                    t, kind = cs[c], ATT[a]["kind"]
                    if kind == SMALL:
                        evacuate(c, f"qT{a}_0", t.qT[:, 0:512], 512, padT_ready)
                        evacuate(c, f"kT{a}_0", t.kT[:, 0:512], 512, padT_ready)
                    elif kind == GQA:
                        for u in range(2):
                            evacuate(c, f"qT3_{u}", t.qT64[:, 512 * u:512 * u + 512], 512, padT_ready)
                        evacuate(c, "kT3_0", t.kT64[:, :], 512, padT_ready)
                    else:
                        for qk, dst in (("q", t.qT), ("k", t.kT)):
                            for j in range(4):
                                evacuate(c, f"{qk}T{a}_{j}", dst[0:96, 512 * j:512 * j + 512], 512,
                                         padT_ready, n=96)

                def probs(c, a):
                    t, nk = cs[c], ATT[a]["nk"]
                    for j in range(4):
                        name = f"sT{a}_{j}"
                        act.wait_ge(filled(c, name), filled_count(it, name))
                        act.activation(t.probs[0:nk, 512 * j:512 * j + 512], bank(c, name)[0:nk, :], ACT.Exp,
                                       scale=ATT[a]["scale"]).then_inc(probs_ready[c], 1)

                def up(c, n):
                    t = cs[c]
                    if n == 2:
                        act.wait_ge(filled(c, "gate2"), filled_count(it, "gate2"))
                        act.activation(t.gate, bank(c, "gate2")[:, :], ACT.Silu).then_inc(act_hidden[c], 1)
                        return
                    act.wait_ge(filled(c, f"up{n}"), filled_count(it, f"up{n}"))
                    for m in range(4):
                        act.activation(t.hid[:, 128 * m:128 * m + 128], bank(c, f"up{n}")[:, 128 * m:128 * m + 128],
                                       ACT.Relu if n == 0 else ACT.Gelu_apprx_tanh,
                                       bias=mlp_bias[:, n, m:m + 1]).then_inc(act_hidden[c], 1)

                for st in STAGES:
                    for c in range(NC):
                        if st[0] == "inputs":
                            to_features(c, 0)
                            to_features(c, 1)
                        elif st[0] == "project":
                            project(c, st[1])
                        elif st[0] == "stack":
                            stack(c, st[1])
                        elif st[0] == "max":
                            evacuate(c, f"nm{st[1]}", cs[c].nmT[:, :], 128, nmT_ready)
                        elif st[0] == "probs":
                            probs(c, st[1])
                        elif st[0] == "outT":
                            a = st[1]
                            n = NH * ATT[a]["hd"] // 128
                            for u in range(AOT_UNITS[a]):
                                width = 128 * (min(n, 4 * u + 4) - 4 * u)
                                evacuate(c, f"oT{a}_{u}", cs[c].aoT[:, 512 * u:512 * u + width], width, aoT_ready)
                        elif st[0] == "apply" and st[1] in NORM_FEAT:
                            to_features(c, NORM_FEAT[st[1]])
                        elif st[0] == "copyT":
                            to_features(c, 8)
                        elif st[0] == "up":
                            up(c, st[1])

        @block.gpsimd
        def _(pool):
            pool.memset(W0[:, :, :], 0.0).then_inc(zeroed, 1)
            for c in range(NC):
                pool.memset(cs[c].c_in[:, :], 0.0).then_inc(zeroed, 1)
            pool.memset(minus_half[:, :], -0.5).then_inc(pool_step, 1)
            pool.wait_ge(pool_step, 1)
            pool.wait_ge(weights_in, 16 * (len(vec_loads) + N_DIAG))
            with pool.Fori(0, ITERS) as it:

                def inverse_std(c, n):
                    pool.wait_ge(stats_ready[c], nth(it, "stats_ready", n + 1))
                    pool.tensor_tensor(cs[c].rstd[:, :], cs[c].var[:, :], minus_half[:, :],
                                       ALU.pow).then_inc(rstd_ready[c], 1)

                def turned(c, a):
                    t, hd = cs[c], ATT[a]["hd"]
                    if ATT[a]["kind"] == SMALL:
                        pool.wait_ge(raw8_ready[c], nth(it, "raw8_ready", a))
                        width, tab, halves = 256, "sin8", "(h t f) -> p h t f"
                    else:
                        pool.wait_ge(raw_ready[c], nth(it, "raw_ready", sum(RAW_UNITS[:a + 1])))
                        width, tab = (1280, "sin64") if a == 3 else (1024, "sin32")
                    n = width // hd
                    if ATT[a]["kind"] == WIDE:
                        src = t.raw[:, 0:width].rearrange("p (h f t) -> p h f t", h=n, t=2)
                        dst = t.turn[:, 0:width].rearrange("p (h f t) -> p h f t", h=n, t=2)
                        sn = table(tab).rearrange("p (f t) -> p f t", t=2)
                        parts = [(dst[:, :, :, i], src[:, :, :, 1 - i], sn[:, :, i]) for i in range(2)]
                        m = hd // 2
                    else:
                        src = t.raw[:, 0:width].rearrange("p (h t f) -> p h t f", h=n, t=2)
                        dst = t.turn[:, 0:width].rearrange("p (h t f) -> p h t f", h=n, t=2)
                        sn = table(tab).rearrange("p (t f) -> p t f", t=2)
                        parts = [(dst[:, :, i, :], src[:, :, 1 - i, :], sn[:, i, :]) for i in range(2)]
                        m = hd // 2
                    for i, (d, s_, k) in enumerate(parts):
                        ins_ = pool.tensor_tensor(d, s_, k.unsqueeze(1).broadcast_to([128, n, m]), ALU.mult)
                    ins_.then_inc(rot_ready[c], 1)

                for st in STAGES:
                    for c in range(NC):
                        if st[0] == "inputs":
                            inverse_std(c, 0)
                        elif st[0] == "stats":
                            inverse_std(c, st[1])
                        elif st[0] == "project" and st[1] > 0:
                            turned(c, st[1])

        @block.vector
        def _(dve):
            links = [0]

            dve.wait_ge(weights_in, 16 * (len(vec_loads) + N_DIAG))
            for c in range(NC):
                t = cs[c]
                dve.memset(t.q8[:, :, 3, :], 0.0).then_inc(dve_step, 1)
                dve.memset(t.k8[:, :, 3, :], 0.0).then_inc(dve_step, 1)
                dve.memset(t.mask8[:, :], 0.0).then_inc(dve_step, 1)
                dve.memset(t.pads[:, :, :, :, :], 0.0).then_inc(dve_step, 1)
                for a in V_OF:
                    dve.memset(v_tile(c, a)[:, :], 0.0).then_inc(dve_step, 1)
            CLEARED = NC * (4 + len(V_OF))
            dve.wait_ge(dve_step, CLEARED)
            for c in range(NC):
                dve.memset(cs[c].q8[:, :, 3, 0:1], 1.0).then_inc(dve_step, 1)
                for a in V_OF:
                    hd = ATT[a]["hd"]
                    dve.memset(v_heads(c, a)[:, :, hd:hd + 1], 1.0).then_inc(dve_step, 1)
            dve.tensor_copy(ident_r[:, :], ident).then_inc(dve_step, 1)
            dve.tensor_copy(causal_r[:, :], table("causal")).then_inc(dve_step, 1)
            dve.tensor_copy(sel_r[:, :], table("selector")).then_inc(dve_step, 1)
            dve.memset(sel1_r[:, :].bitcast(F32), 0.0).then_inc(dve_step, 1)
            ONCE = CLEARED + NC * (1 + len(V_OF)) + 5
            dve.wait_ge(dve_step, ONCE - 1)
            dve.tensor_copy(sel1_r[0:32, :], table("selector")[0:32, :]).then_inc(dve_step, 1)
            dve.wait_ge(dve_step, ONCE)
            dve.sem_inc(consts_set, 1)

            with dve.Fori(0, ITERS) as it:

                def step(ins):
                    ins.then_inc(dve_step, 1)
                    links[0] += 1

                def settle(apart=False):
                    dve.wait_ge(dve_step, it * DVE_STEPS + (ONCE + links[0]))
                    if apart:
                        dve.memset(wait_carrier[:, :], 0.0)

                def link(ins, apart=False):
                    step(ins)
                    settle(apart)

                def statistics(c, n, src):
                    t = cs[c]
                    kind, eps, _, _ = NORM[n]
                    link(dve.bn_stats(t.stats[:, :], src), apart=True)
                    link(dve.bn_aggr(t.mv[:, :], t.stats[:, :]))
                    if kind == "rms":
                        link(dve.scalar_tensor_tensor(t.var[:, :], t.mv[:, 0:1], t.mv[:, 0:1], t.mv[:, 1:2],
                                                      ALU.mult, ALU.add))
                        dve.tensor_scalar(t.var[:, :], t.var[:, :], eps, None,
                                          ALU.add).then_inc(stats_ready[c], 1)
                    else:
                        dve.tensor_scalar(t.var[:, :], t.mv[:, 1:2], eps, None,
                                          ALU.add).then_inc(stats_ready[c], 1)

                def apply(c, n):
                    t = cs[c]
                    kind, _, g, b = NORM[n]
                    dve.wait_ge(rstd_ready[c], nth(it, "rstd_ready", n + 1))
                    if kind == "rms":
                        src, dst = (t.c_in, t.cn) if n == 0 else (t.x, t.xn)
                        dve.tensor_scalar(dst[:, :], src[:, :], t.rstd[:, :], None,
                                          ALU.mult).then_inc(tok_ready[c], 1)
                    elif kind == "pre":
                        dve.tensor_scalar(t.xn[:, :], t.x[:, :], t.mv[:, 0:1], t.rstd[:, :],
                                          ALU.subtract, ALU.mult).then_inc(tok_ready[c], 1)
                    else:
                        link(dve.tensor_scalar(t.xn[:, :], t.x[:, :], t.mv[:, 0:1], t.rstd[:, :],
                                               ALU.subtract, ALU.mult))
                        link(dve.tensor_tensor(t.xn[:, :], t.xn[:, :], row(g), ALU.mult))
                        if n == 10:
                            dve.wait_ge(stored[c], it * 16 + 16)
                            dve.tensor_tensor(t.y[:, :], t.xn[:, :], row(b),
                                              ALU.add).then_inc(out_ready[c], 1)
                        else:
                            ins_ = dve.tensor_tensor(t.x[:, :], t.xn[:, :], row(b), ALU.add)
                            if n == 2:
                                link(ins_)
                            else:
                                ins_.then_inc(tok_ready[c], 1)

                def add_to_x(c, name, bias, first=False, tok=False):
                    t = cs[c]
                    dve.wait_ge(filled(c, name), filled_count(it, name))
                    ins_ = dve.tensor_tensor(t.x[:, :], bank(c, name)[:, 0:128],
                                             t.x_in[:, :] if first else t.x[:, :], ALU.add)
                    ins_.then_inc(added[c], 1)
                    dve.wait_ge(reader(c, name), read_count(it, name))
                    if bias:
                        ins_ = dve.tensor_tensor(t.x[:, :], t.x[:, :], row(bias), ALU.add)
                        if first:
                            ins_.then_inc(inputs_used[c], 1)
                            dve.wait_ge(inputs_used[c], nth(it, "inputs_used", 1))
                        else:
                            link(ins_)

                def inputs(c):
                    t = cs[c]
                    dve.wait_ge(loaded[c], it * (16 * N_LOADS) + 16 * N_LOADS)
                    statistics(c, 0, t.c_in[:, :])
                    link(dve.tensor_scalar(t.zero[0:SK, :], t.key_mask[0:SK, :], 0.0, None, ALU.is_equal))
                    step(dve.tensor_scalar(t.keep[0:SK, :], t.zero[0:SK, :], -1.0, 1.0, ALU.mult, ALU.add))
                    step(dve.tensor_scalar(t.kbias[0:SK, :], t.zero[0:SK, :], -1e20, None, ALU.mult))
                    link(dve.tensor_scalar(t.mask8[:, 0:SK], t.mask_in[:, :], 8.0, -3e38, ALU.mult, ALU.max))
                    link(dve.tensor_copy(t.mask_hi[:, :], t.mask8[:, :]))
                    step(dve.tensor_tensor(t.mask_lo[:, :], t.mask8[:, :], t.mask_hi[:, :].bitcast(F32), ALU.subtract))
                    apply(c, 0)

                def project(c, a):
                    t = cs[c]
                    if ATT[a]["kind"] != SMALL:
                        return
                    name = f"qkv{a}"
                    dve.wait_ge(filled(c, name), filled_count(it, name))
                    src = bank(c, name)
                    if a == 0:
                        step(dve.tensor_copy(t.raw[:, 0:256], src[:, 0:256]))
                        dve.tensor_copy(v_heads(c, a)[:, :, 0:8],
                                        src[0:SK, 256:384].rearrange("p (h d) -> p h d", h=NH)).then_inc(qkv_read[c], 1)
                        dve.wait_ge(reader(c, name), read_count(it, name))
                        link(dve.tensor_scalar(t.raw[0:SK, 128:256], t.raw[0:SK, 128:256], t.keep[0:SK, :], None,
                                               ALU.mult))
                        return
                    i = ROWS.index("L1_sa_bq" if a == 1 else "L1_ca_bq")
                    dve.tensor_tensor(t.raw[:, 0:256], src[:, 0:256],
                                      rows[:, i:i + 2, :].rearrange("p a n -> p (a n)"),
                                      ALU.add).then_inc(raw8_ready[c], 1)
                    nk = ATT[a]["nk"]
                    dve.tensor_tensor(v_heads(c, a)[:, :, 0:8],
                                      src[0:nk, 256:384].rearrange("p (h d) -> p h d", h=NH),
                                      rows[0:nk, i + 2, :].rearrange("p (h d) -> p h d", h=NH),
                                      ALU.add).then_inc(qkv_read[c], 1)
                    dve.wait_ge(raw8_ready[c], nth(it, "raw8_ready", a))

                def turn(c, a):
                    t, hd = cs[c], ATT[a]["hd"]
                    if a == 0:
                        return
                    width = {SMALL: 256, GQA: 1280, WIDE: 1024}[ATT[a]["kind"]]
                    n = width // hd
                    dve.wait_ge(rot_ready[c], nth(it, "rot_ready", a))
                    raw = t.raw[:, 0:width].rearrange("p (h d) -> p h d", h=n)
                    link(dve.tensor_tensor(raw, raw, table(f"cos{hd}").unsqueeze(1).broadcast_to([128, n, hd]),
                                           ALU.mult))
                    link(dve.tensor_tensor(t.raw[:, 0:width], t.raw[:, 0:width], t.turn[:, 0:width], ALU.add))

                def stack(c, a):
                    t, kind = cs[c], ATT[a]["kind"]
                    if kind == GQA:
                        k = t.raw[:, 1024:1280].rearrange("p (h d) -> p h d", h=4)
                        dup = t.kdup.rearrange("p (h r d) -> p h r d", h=4, r=2)
                        dve.tensor_copy(dup, k.unsqueeze(2).broadcast_to([128, 4, 2, 64])
                                        ).then_inc(pads_ready[c], 1)
                        return
                    hd = ATT[a]["hd"]
                    n = NH * hd
                    q = t.raw[:, 0:n].rearrange("p (h d) -> p h d", h=NH)
                    k = t.raw[:, n:2 * n].rearrange("p (h d) -> p h d", h=NH)
                    q_to, k_to = (t.q8, t.k8) if kind == SMALL else (t.pads[:, 0], t.pads[:, 1])
                    if kind == SMALL:
                        if a == 0:
                            step(dve.tensor_copy(t.k8[0:SK, :, 3, 0:1],
                                                 t.kbias[0:SK, :].unsqueeze(1).broadcast_to([SK, NH, 1])))
                        elif a == 1:
                            step(dve.memset(t.k8[:, :, 3, 0:1], 0.0))
                    step(dve.tensor_copy(q_to[:, :, 0:2, :].bitcast(F32R), q.unsqueeze(2).broadcast_to([128, NH, 2, hd])))
                    link(dve.tensor_copy(k_to[:, :, 0:3:2, :].bitcast(F32R),
                                         k.unsqueeze(2).broadcast_to([128, NH, 2, hd])))
                    step(dve.tensor_tensor(q_to[:, :, 2, :], q, q_to[:, :, 0, :], ALU.subtract))
                    dve.tensor_tensor(k_to[:, :, 1, :], k, k_to[:, :, 0, :],
                                      ALU.subtract).then_inc(pads_ready[c], 1)

                def scores(c, a):
                    t, nk = cs[c], ATT[a]["nk"]
                    nke = S if nk == S else SKE
                    for j in range(4):
                        name = f"s{a}_{j}"
                        dve.wait_ge(filled(c, name), filled_count(it, name))
                        src = bank(c, name)[:, 0:4 * nke].rearrange("p (h k) -> p h k", h=4)[:, :, 0:nk]
                        dve.tensor_reduce(t.nmax[:, 4 * j:4 * j + 4], src, AX.X, ALU.max,
                                          negate=True).then_inc(score_read[c], 1)
                    dve.wait_ge(reader(c, name), read_count(it, name))
                    nm = t.nmax[:, :].unsqueeze(1).broadcast_to([128, 4, NH])
                    link(dve.tensor_copy(t.nm[:, :, 0, :].bitcast(F32R), nm))
                    dve.tensor_tensor(t.nm[:, :, 1, :], nm, t.nm[:, :, 0, :],
                                      ALU.subtract).then_inc(nm_ready[c], 1)

                def values(c, a):
                    t, kind, hd = cs[c], ATT[a]["kind"], ATT[a]["hd"]
                    units = PV_UNITS[kind]
                    per = NH // units
                    for u in range(units):
                        name = f"pv{a}_{u}"
                        dve.wait_ge(filled(c, name), filled_count(it, name))
                        src = bank(c, name)[:, 0:per * (hd + 1)].rearrange("p (h d) -> p h d", h=per)
                        rs = t.rsum[:, u * per:(u + 1) * per].unsqueeze(2)
                        link(dve.reciprocal(rs, src[:, :, hd:hd + 1]))
                        dst = t.ao[:, u * per * hd:(u + 1) * per * hd].rearrange("p (h d) -> p h d", h=per)
                        dve.tensor_tensor(dst, src[:, :, 0:hd], rs.broadcast_to([128, per, hd]),
                                          ALU.mult).then_inc(ao_ready[c], 1)

                def up2(c):
                    t = cs[c]
                    dve.wait_ge(act_hidden[c], nth(it, "act_hidden", sum(HID_UNITS[:3])))
                    dve.wait_ge(filled(c, "up2"), filled_count(it, "up2"))
                    dve.tensor_tensor(t.hid, bank(c, "up2")[:, :], t.gate,
                                      ALU.mult).then_inc(hidden2_ready[c], 1)

                OUT_BIAS = ["L0_b_out", "L1_sa_bo", "L1_ca_bo", None, None, None]
                DOWN_BIAS = ["L0_b_ff2", "L1_fc2_b", None, "L3_b_ff2"]
                for st in STAGES:
                    for c in range(NC):
                        if st[0] == "inputs":
                            inputs(c)
                        elif st[0] == "project":
                            project(c, st[1])
                        elif st[0] == "turn":
                            turn(c, st[1])
                        elif st[0] == "stack":
                            stack(c, st[1])
                        elif st[0] == "scores":
                            scores(c, st[1])
                        elif st[0] == "values":
                            values(c, st[1])
                        elif st[0] == "out":
                            add_to_x(c, f"y{st[1]}", OUT_BIAS[st[1]], first=st[1] == 0)
                        elif st[0] == "stats":
                            statistics(c, st[1], cs[c].x[:, :])
                        elif st[0] == "apply":
                            apply(c, st[1])
                        elif st == ("up", 2):
                            up2(c)
                        elif st[0] == "down":
                            add_to_x(c, f"down{st[1]}", DOWN_BIAS[st[1]])
                        elif st[0] == "copyT":
                            dve.sem_inc(tok_ready[c], 1)
                assert links[0] == DVE_STEPS, ("DVE_STEPS", links[0])



def host_constants():
    import numpy as np

    at = np.arange(S)
    c = {"ident": np.eye(S), "causal": np.where(at[None, :] <= at[:, None], 0.0, -2.0 ** 100)}
    r = np.arange(128) % 16
    c["selector"] = (r[:, None] == np.arange(NH)[None, :]).astype(np.float64)
    for hd, pairs in ((8, False), (64, False), (32, True)):
        inv = (np.float32(1.0) / np.power(np.float32(10000.0), np.arange(0, hd, 2, dtype=np.float32) / np.float32(hd)))
        f = at.astype(np.float32)[:, None] * inv.astype(np.float32)[None, :]
        cos, sin = np.cos(f), np.sin(f)
        if pairs:
            c[f"cos{hd}"] = np.repeat(cos, 2, axis=1)
            c[f"sin{hd}"] = np.stack([-sin, sin], axis=-1).reshape(S, hd)
        else:
            c[f"cos{hd}"] = np.concatenate([cos, cos], axis=1)
            c[f"sin{hd}"] = np.concatenate([-sin, sin], axis=1)
    return np.ascontiguousarray(np.concatenate([c[n] for n in HOST], axis=1).astype(np.float32))


def kernel(**inputs):
    import numpy as np
    import concourse.bacc as bacc
    from concourse.bass_utils import run_bass_kernel_spmd

    nc = bacc.Bacc("TRN2", target_bir_lowering=False, num_devices=1)
    arrays, aps = {}, {}
    for name, value in inputs.items():
        a = np.ascontiguousarray(value)
        arrays[f"in_{name}"] = a
        aps[name] = nc.dram_tensor(f"in_{name}", a.shape, mybir.dt.from_np(a.dtype), kind="ExternalInput").ap()
    k = host_constants()
    arrays["constants"] = k
    kap = nc.dram_tensor("constants", k.shape, F32, kind="ExternalInput").ap()
    out = nc.dram_tensor("out", (B, S, E), F32, kind="ExternalOutput").ap()
    build(nc, aps, kap, out)
    r = run_bass_kernel_spmd(nc, [arrays], core_ids=[0])
    return r.results[0]["out"]
```

```python
from contextlib import ExitStack

import concourse.bass as bass
import concourse.mybir as mybir

F32 = mybir.dt.float32
F32R = mybir.dt.float32r
I32 = mybir.dt.int32
ALU = mybir.AluOpType
ACT = mybir.ActivationFunctionType
AX = mybir.AxisListType

B, S, E, SK = 64, 128, 128, 77
NH, FF = 16, 512
SKE = SK + 1
NC = 2
ITERS = B // NC
NBANK = 4
PV_N = 128

SMALL, WIDE, GQA = "small", "wide", "gqa"
KINDS = [SMALL, WIDE, GQA]
ATT = [
    dict(kind=SMALL, hd=8, nk=SK, scale=128 ** -0.5, bias=None),
    dict(kind=SMALL, hd=8, nk=S, scale=8 ** -0.5, bias="causal"),
    dict(kind=SMALL, hd=8, nk=SK, scale=8 ** -0.5, bias=None),
    dict(kind=GQA, hd=64, nk=SK, scale=0.125, bias="mask"),
    dict(kind=WIDE, hd=32, nk=S, scale=32 ** -0.5, bias=None),
    dict(kind=WIDE, hd=32, nk=SK, scale=32 ** -0.5, bias=None),
]


def head_of(kind, j, p):
    if kind == SMALL:
        return 4 * p + j
    if kind == GQA:
        return 2 * (4 * (j // 2) + p) + j % 2
    return 4 * j + p


PV_UNITS = {SMALL: 1, GQA: 4, WIDE: 2}


def bank_plan():
    plan = [("xc_T", "feat_ready", 1)]

    def add(event, n, *names):
        plan.extend((name, event, n) for name in names)

    def attention(a):
        kind = ATT[a]["kind"]
        if kind == SMALL:
            add("qkv_read", 1, f"qkv{a}")
            add("padT_ready", 1, f"qT{a}_0")
            add("kT_ready", 1, f"kT{a}_0")
        elif kind == GQA:
            add("raw_ready", 1, f"q{a}_0", f"q{a}_1")
            add("raw_ready", 2, f"kv{a}")
            add("padT_ready", 1, f"qT{a}_0", f"qT{a}_1", f"kT{a}_0")
        else:
            add("raw_ready", 1, f"q{a}_0", f"k{a}", f"v{a}")
            add("padT_ready", 1, *[f"qT{a}_{j}" for j in range(4)])
            add("kT_ready", 1, *[f"kT{a}_{j}" for j in range(4)])
        add("score_read", 1, *[f"s{a}_{j}" for j in range(4)])
        add("nmT_ready", 1, f"nm{a}")
        add("probs_ready", 1, *[f"sT{a}_{j}" for j in range(4)])
        add("ao_ready", 1, *[f"pv{a}_{u}" for u in range(PV_UNITS[kind])])
        if a == 0:
            add("feat_ready", 1, "cn_T")
        add("aoT_ready", 1, *[f"oT{a}_{u}" for u in range(2 if kind == GQA else 1)])
        add("added", 1, f"y{a}")

    def mlp(n):
        add("feat_ready", 1, f"h_T{n}")
        if n == 2:
            add("act_hidden", 1, "gate2")
            add("hidden2_ready", 1, "up2")
        else:
            add("act_hidden", 4, f"up{n}")
        add("added", 1, f"down{n}")

    attention(0)
    mlp(0)
    add("feat_ready", 1, "a_T1")
    attention(1)
    add("feat_ready", 1, "a_T2")
    attention(2)
    mlp(1)
    add("feat_ready", 1, "a_T3")
    attention(3)
    mlp(2)
    add("feat_ready", 1, "a_T4")
    attention(4)
    add("feat_ready", 1, "a_T5")
    attention(5)
    mlp(3)
    return plan


PLAN = bank_plan()
NAMES = [name for name, _, _ in PLAN]
PLACE = {name: (n % NBANK, n // NBANK) for n, name in enumerate(NAMES)}
USES = [sum(1 for n in range(len(PLAN)) if n % NBANK == b) for b in range(NBANK)]
PER_ITER = {
    "stats_ready": 11, "rstd_ready": 11, "tok_ready": 10, "pads_ready": 10, "raw8_ready": 2,
    "rot_ready": 9, "roped": 4, "hi_ready": 4, "nm_ready": 6, "inputs_used": 1, "out_ready": 1,
}
READ_AT = {}
for _name, _event, _n in PLAN:
    PER_ITER[_event] = PER_ITER.get(_event, 0) + _n
    READ_AT[_name] = (_event, PER_ITER[_event])


def before(name):
    b, k = PLACE[name]
    at = NBANK * (k - 1) + b if k else NBANK * (USES[b] - 1) + b
    return NAMES[at], k == 0


STREAM = {"inputs": 7, "stack": [12] * 6, "max": [5] * 6, "apply": [8] * 7 + [0] + [8] * 3, "down": [1] * 4}
V_OF = (1, 2, 3, 4, 5)
DVE_STEPS = 178

COLS = ["L1_ln1_g", "L1_ln1_b", "L1_ln2_g", "L1_ln2_b", "L1_ln3_g", "L1_ln3_b", "L2_ln1_w", "L2_ln2_w"]
ROWS = (["L1_sa_bq", "L1_sa_bk", "L1_sa_bv", "L1_ca_bq", "L1_ca_bk", "L1_ca_bv",
         "L0_b_out", "L1_sa_bo", "L1_ca_bo", "L0_b_ff2", "L1_fc2_b", "L3_b_ff2",
         "L0_g1", "L0_beta1", "L0_g2", "L0_beta2",
         "L3_g1", "L3_be1", "L3_g2", "L3_be2", "L3_g3", "L3_be3"])
MLP_BIAS = ["L0_b_ff1", "L1_fc1_b", None, "L3_b_ff1"]
HOST = ["ident", "causal", "selector", "cos8", "sin8", "cos64", "sin64", "cos32", "sin32"]
HOST_W = {"ident": S, "causal": S, "selector": 24, "cos8": 8, "sin8": 8, "cos64": 64, "sin64": 64,
          "cos32": 32, "sin32": 32}
HOST_AT = {n: sum(HOST_W[m] for m in HOST[:i]) for i, n in enumerate(HOST)}
HOST_N = sum(HOST_W.values())


def build(nc, ins, consts, out):
    nc.disable_value_cache = True
    ctx = ExitStack()
    with ctx:
        def sb(name, shape, dt=F32):
            return ctx.enter_context(nc.sbuf_tensor(name, shape, dt))

        def sem(name):
            return ctx.enter_context(nc.semaphore(name))

        w_in = {n[:2] + n[8:] if n[0] == "L" else n: ap for n, ap in ins.items()}

        def blocks(name, rows):
            return w_in[name].rearrange("(m p) n -> p m n", p=128) if rows > 128 else w_in[name]

        W0 = sb("W0", [128, 3, 128])
        W0o = sb("W0o", [128, 1, 128])
        W1s = sb("W1s", [128, 3, 128])
        W1so = sb("W1so", [128, 1, 128])
        W1c = sb("W1c", [128, 3, 128])
        W1co = sb("W1co", [128, 1, 128])
        W2q = sb("W2q", [128, 1024])
        W2kv = sb("W2kv", [128, 512])
        W2o = sb("W2o", [128, 8, 128])
        W4 = sb("W4", [128, 1536])
        W4o = sb("W4o", [128, 4, 128])
        W5 = sb("W5", [128, 3, 512])
        W5o = sb("W5o", [128, 4, 128])
        Wup = [sb(f"Wup{n}", [128, FF]) for n in range(4)]
        Wgate = sb("Wgate", [128, FF])
        Wdown = [sb(f"Wdown{n}", [128, 4, 128]) for n in range(4)]
        Wo = [W0o, W1so, W1co, W2o, W4o, W5o]
        cols = sb("cols", [128, len(COLS)])
        mlp_bias = sb("mlp_bias", [128, 4, 4])
        rows = sb("rows", [128, len(ROWS), 128])
        host = sb("host", [128, HOST_N])
        ident_r = sb("ident_r", [128, S], F32R)
        causal_r = sb("causal_r", [128, S], F32R)
        sel_r = sb("sel_r", [128, 12], F32R)
        wait_carrier = sb("wait_carrier", [128, 1])
        minus_half = sb("minus_half", [128, 1])
        ident = host[:, HOST_AT["ident"]:HOST_AT["ident"] + S]

        def row(name):
            return rows[:, ROWS.index(name), :]

        def col(name):
            i = COLS.index(name)
            return cols[:, i:i + 1]

        def table(name):
            return host[:, HOST_AT[name]:HOST_AT[name] + HOST_W[name]]

        class Ctx:
            pass

        cs = []
        for c in range(NC):
            t = Ctx()
            t.x_in = sb(f"x_in{c}", [128, E])
            t.c_in = sb(f"c_in{c}", [128, E])
            t.mask_in = sb(f"mask_in{c}", [128, SK])
            t.key_mask = sb(f"key_mask{c}", [128, 1], I32)
            t.x = sb(f"x{c}", [128, E])
            t.xn = sb(f"xn{c}", [128, E])
            t.cn = sb(f"cn{c}", [128, E])
            t.y = sb(f"y{c}", [128, E])
            t.stats = sb(f"stats{c}", [128, 6])
            t.mv = sb(f"mv{c}", [128, 2])
            t.var = sb(f"var{c}", [128, 1])
            t.rstd = sb(f"rstd{c}", [128, 1])
            t.xcT = sb(f"xcT{c}", [128, 2, 128])
            t.cnT = sb(f"cnT{c}", [128, 128])
            t.hT = sb(f"hT{c}", [128, 128])
            t.zero = sb(f"zero{c}", [128, 1])
            t.keep = sb(f"keep{c}", [128, 1])
            t.kbias = sb(f"kbias{c}", [128, 1])
            t.raw = sb(f"raw{c}", [128, 1280])
            t.q8 = sb(f"q8{c}", [128, NH, 4, 8])
            t.k8 = sb(f"k8{c}", [128, NH, 4, 8])
            t.pads = sb(f"pads{c}", [128, 2, NH, 3, 32])
            t.v8 = {nk: sb(f"v8_{nk}_{c}", [128, NH * 9 + PV_N]) for nk in (S, SK)}
            t.v32 = {nk: sb(f"v32_{nk}_{c}", [128, NH * 33 + PV_N]) for nk in (S, SK)}
            t.v64 = {SK: sb(f"v64_{c}", [128, 4 * 65 + PV_N])}
            t.qT = sb(f"qT{c}", [128, NH * S], F32R)
            t.kT = sb(f"kT{c}", [128, NH * S], F32R)
            t.qT64 = sb(f"qT64{c}", [128, 8 * S])
            t.kT64 = sb(f"kT64{c}", [128, 4 * S])
            t.nmax = sb(f"nmax{c}", [128, NH])
            t.nm = sb(f"nm{c}", [128, 128])
            t.nmT = sb(f"nmT{c}", [128, 4, S], F32R)
            t.mask_hi = sb(f"mask_hi{c}", [128, SKE], F32R)
            t.mask_lo = sb(f"mask_lo{c}", [128, SKE], F32R)
            t.mask8 = sb(f"mask8{c}", [128, SKE])
            t.rsum = sb(f"rsum{c}", [128, NH])
            t.cosd = sb(f"cosd{c}", [128, 1280])
            t.probs = t.pads[:, :, :, :, :].rearrange("p a h s d -> p (a h s d)")[:, 0:NH * S]
            free = t.pads[:, :, :, :, :].rearrange("p a h s d -> p (a h s d)")
            t.turn = {SMALL: t.qT64[:, 0:256], GQA: free[:, 0:1280], WIDE: t.qT64[:, :]}
            t.kdup = free[:, 0:512]
            t.ao = t.raw[:, 0:1024]
            t.aoT = t.qT64[:, :]
            t.hid = t.kT64[:, :]
            t.gate = t.qT64[:, 0:512]
            cs.append(t)
        banks = [[ctx.enter_context(nc.psum_tensor(f"bank{c}_{b}", [128, 512], F32))
                  for b in range(NBANK)] for c in range(NC)]

        weights_in = sem("weights_in")
        consts_set = sem("consts_set")
        zeroed = sem("zeroed")
        dve_step = sem("dve_step")
        pool_step = sem("pool_step")
        loaded = [sem(f"loaded{c}") for c in range(NC)]
        stored = [sem(f"stored{c}") for c in range(NC)]
        full = [[sem(f"full{c}_{b}") for b in range(NBANK)] for c in range(NC)]
        stats_ready = [sem(f"stats_ready{c}") for c in range(NC)]
        rstd_ready = [sem(f"rstd_ready{c}") for c in range(NC)]
        tok_ready = [sem(f"tok_ready{c}") for c in range(NC)]
        feat_ready = [sem(f"feat_ready{c}") for c in range(NC)]
        pads_ready = [sem(f"pads_ready{c}") for c in range(NC)]
        qkv_read = [sem(f"qkv_read{c}") for c in range(NC)]
        raw8_ready = [sem(f"raw8_ready{c}") for c in range(NC)]
        raw_ready = [sem(f"raw_ready{c}") for c in range(NC)]
        rot_ready = [sem(f"rot_ready{c}") for c in range(NC)]
        roped = [sem(f"roped{c}") for c in range(NC)]
        hi_ready = [sem(f"hi_ready{c}") for c in range(NC)]
        kT_ready = [sem(f"kT_ready{c}") for c in range(NC)]
        padT_ready = [sem(f"padT_ready{c}") for c in range(NC)]
        score_read = [sem(f"score_read{c}") for c in range(NC)]
        nm_ready = [sem(f"nm_ready{c}") for c in range(NC)]
        nmT_ready = [sem(f"nmT_ready{c}") for c in range(NC)]
        probs_ready = [sem(f"probs_ready{c}") for c in range(NC)]
        ao_ready = [sem(f"ao_ready{c}") for c in range(NC)]
        aoT_ready = [sem(f"aoT_ready{c}") for c in range(NC)]
        added = [sem(f"added{c}") for c in range(NC)]
        act_hidden = [sem(f"act_hidden{c}") for c in range(NC)]
        hidden2_ready = [sem(f"hidden2_ready{c}") for c in range(NC)]
        inputs_used = [sem(f"inputs_used{c}") for c in range(NC)]
        out_ready = [sem(f"out_ready{c}") for c in range(NC)]
        ev = [dict(
            stats_ready=stats_ready[c],
            rstd_ready=rstd_ready[c],
            tok_ready=tok_ready[c],
            feat_ready=feat_ready[c],
            pads_ready=pads_ready[c],
            qkv_read=qkv_read[c],
            raw8_ready=raw8_ready[c],
            raw_ready=raw_ready[c],
            rot_ready=rot_ready[c],
            roped=roped[c],
            hi_ready=hi_ready[c],
            kT_ready=kT_ready[c],
            padT_ready=padT_ready[c],
            score_read=score_read[c],
            nm_ready=nm_ready[c],
            nmT_ready=nmT_ready[c],
            probs_ready=probs_ready[c],
            ao_ready=ao_ready[c],
            aoT_ready=aoT_ready[c],
            added=added[c],
            act_hidden=act_hidden[c],
            hidden2_ready=hidden2_ready[c],
            inputs_used=inputs_used[c],
            out_ready=out_ready[c],
        ) for c in range(NC)]

        def nth(it, name, n):
            return it * PER_ITER[name] + (PER_ITER[name] + n)

        def filled_count(it, name):
            b, k = PLACE[name]
            return it * USES[b] + (k + 1)

        def reader(c, name):
            return ev[c][READ_AT[name][0]]

        def read_count(it, name):
            return nth(it, *READ_AT[name])

        def last_reader(c, name):
            return reader(c, before(name)[0])

        def last_read_count(it, name):
            held, earlier = before(name)
            event, n = READ_AT[held]
            return nth(it, event, n - PER_ITER[event] if earlier else n)

        def v_tile(c, a):
            t, kind, nk = cs[c], ATT[a]["kind"], ATT[a]["nk"]
            return (t.v8 if kind == SMALL else t.v32 if kind == WIDE else t.v64)[nk]

        def v_heads(c, a):
            nk, hd = ATT[a]["nk"], ATT[a]["hd"]
            n = 4 if ATT[a]["kind"] == GQA else NH
            return v_tile(c, a)[0:nk, 0:n * (hd + 1)].rearrange("p (h d) -> p h d", h=n)

        def bank(c, name):
            return banks[c][PLACE[name][0]]

        def filled(c, name):
            return full[c][PLACE[name][0]]

        N_LOADS = 4
        vec_loads = []
        for i, (w, names) in enumerate([(W0o, ["L0_w_out"]), (W1so, ["L1_sa_wo"]), (W1co, ["L1_ca_wo"])]):
            vec_loads.append((w[:, 0, :], w_in[names[0]]))
        for w, names in ((W1s, ["L1_sa_wq", "L1_sa_wk", "L1_sa_wv"]), (W1c, ["L1_ca_wq", "L1_ca_wk", "L1_ca_wv"]),
                         (W5, ["L3_w_q", "L3_w_k", "L3_w_v"])):
            for i, n in enumerate(names):
                vec_loads.append((w[:, i, :], w_in[n]))
        vec_loads += [
            (W2q[:, :], w_in["L2_Wq"]), (W2kv[:, 0:256], w_in["L2_Wk"]), (W2kv[:, 256:512], w_in["L2_Wv"]),
            (W2o[:, :, :], blocks("L2_Wo", 1024)), (W4[:, :], w_in["L3_w_qkv"]),
            (W4o[:, :, :], blocks("L3_w_out1", 512)), (W5o[:, :, :], blocks("L3_w_out2", 512)),
            (Wup[0][:, :], w_in["L0_w_ff1"]), (Wup[1][:, :], w_in["L1_fc1_w"]),
            (Wup[2][:, :], w_in["L2_Wup"]), (Wup[3][:, :], w_in["L3_w_ff1"]), (Wgate[:, :], w_in["L2_Wgate"]),
            (Wdown[0][:, :, :], blocks("L0_w_ff2", 512)), (Wdown[1][:, :, :], blocks("L1_fc2_w", 512)),
            (Wdown[2][:, :, :], blocks("L2_Wdown", 512)), (Wdown[3][:, :, :], blocks("L3_w_ff2", 512)),
            (host[:, :], consts),
        ]
        for i, n in enumerate(COLS):
            vec_loads.append((cols[:, i:i + 1], w_in[n].rearrange("(p o) -> p o", o=1)))
        for i, n in enumerate(ROWS):
            vec_loads.append((rows[:, i, :], w_in[n].rearrange("(o n) -> o n", o=1).broadcast_to([128, 128])))
        for i, n in enumerate(MLP_BIAS):
            if n:
                vec_loads.append((mlp_bias[:, i, :], w_in[n].rearrange("(m p) -> p m", p=128)))
        N_DIAG = 3 * NH

        ctx.enter_context(nc.allow_non_contiguous_dma(reason="vectors, once, and the key mask"))
        block = ctx.enter_context(nc.Block())

        @block.sync
        def _(sp):
            for dst, src in vec_loads:
                sp.dma_start(dst, src).then_inc(weights_in, 16)
            sp.wait_ge(zeroed, 1 + NC)
            for i, n in enumerate(("L0_wq", "L0_wk", "L0_wv")):
                for h in range(NH):
                    sp.dma_start(W0[8 * h:8 * h + 8, i, 8 * h:8 * h + 8], w_in[n]).then_inc(weights_in, 16)

            def load(c, b):
                t = cs[c]
                sp.dma_start(t.x_in[:, :], w_in["x"][b]).then_inc(loaded[c], 16)
                sp.dma_start(t.c_in[0:SK, :], w_in["ctx_1024"][b]).then_inc(loaded[c], 16)
                sp.dma_start(t.mask_in[:, :], w_in["mask_Bx1xSxS2_ff0"][b, 0]).then_inc(loaded[c], 16)
                sp.dma_start(t.key_mask[0:SK, :],
                             w_in["mask_Bx1x1xS2_if1"][b, 0].rearrange("o k -> k o")).then_inc(loaded[c], 16)

            for c in range(NC):
                load(c, c)
            for c in range(NC):
                sp.sem_inc(stored[c], 16)
            with sp.Fori(0, ITERS - 1) as it:
                used = [sp.snap(it * PER_ITER["inputs_used"] + (PER_ITER["inputs_used"] + 1)) for c in range(NC)]
                ready = [sp.snap(it * PER_ITER["out_ready"] + (PER_ITER["out_ready"] + 1)) for c in range(NC)]
                for c in range(NC):
                    sp.wait_ge(inputs_used[c], used[c])
                    load(c, it * NC + (NC + c))
                for c in range(NC):
                    sp.wait_ge(out_ready[c], ready[c])
                    sp.dma_start(out[it * NC + c], cs[c].y[:, :]).then_inc(stored[c], 16)
            for c in range(NC):
                sp.wait_ge(out_ready[c], (ITERS + 1) * PER_ITER["out_ready"])
                sp.dma_start(out[(ITERS - 1) * NC + c], cs[c].y[:, :]).then_inc(stored[c], 16)
            for c in range(NC):
                sp.wait_ge(stored[c], 16 * (ITERS + 1))

        def both(*stages):
            return [(c, st) for c in range(NC) for st in stages]

        def attention(a):
            def quarters(c, name, *which):
                return [(c, (name, a, i)) for i in which]

            context = both(("stats", 0)) + both(("mask",), ("apply", 0)) if a == 0 else []
            context_T = both(("contextT",)) if a == 0 else []
            ahead = both(("project", a)) + both(("turn", a)) + both(("stack", a)) + both(("stack_k", a))
            scores = (quarters(0, "scores", 0, 1, 2, 3) + quarters(1, "scores", 0) + [(0, ("max", a))]
                      + quarters(1, "scores", 1, 2, 3))
            values = (quarters(0, "values", 0, 1, 2, 3) + quarters(1, "values", 0, 1)
                      + context_T[0:1] + [(0, ("outT", a))] + quarters(1, "values", 2, 3) + context_T[1:2])
            return (ahead + scores + quarters(0, "probs", 0) + [(1, ("max", a))] + quarters(0, "probs", 1, 2, 3)
                    + quarters(1, "probs", 0, 1, 2, 3) + context + values)

        def attention_and_norm(a, n):
            return (attention(a) + [(0, ("out", a)), (0, ("stats", n)), (1, ("outT", a)), (1, ("out", a)),
                                    (1, ("stats", n))] + both(("apply", n)))

        def mlp_and_norm(m, n):
            return both(("up", m)) + both(("down", m), ("stats", n)) + both(("apply", n))

        ORDER = (both(("inputs",)) + attention_and_norm(0, 1) + mlp_and_norm(0, 2) + both(("stats", 3), ("apply", 3))
                 + attention_and_norm(1, 4) + attention_and_norm(2, 5) + mlp_and_norm(1, 6)
                 + attention_and_norm(3, 7) + both(("up", 2)) + both(("down", 2)) + both(("copyT",))
                 + attention_and_norm(4, 8) + attention_and_norm(5, 9) + mlp_and_norm(3, 10))

        class Turn:
            it, steps = None, 0

        def in_turn(eng, now, run):
            with eng.Fori(0, ITERS) as it:
                now.it = it
                for c, st in ORDER:
                    run(st, c)

        NORM = {0: ("rms", 1e-6, "L2_ln1_w", None), 1: ("post", 1e-5, "L0_g1", "L0_beta1"),
                2: ("post", 1e-5, "L0_g2", "L0_beta2"), 3: ("pre", 1e-5, "L1_ln1_g", "L1_ln1_b"),
                4: ("pre", 1e-5, "L1_ln2_g", "L1_ln2_b"), 5: ("pre", 1e-5, "L1_ln3_g", "L1_ln3_b"),
                6: ("rms", 1e-6, "L2_ln1_w", None), 7: ("rms", 1e-6, "L2_ln2_w", None),
                8: ("post", 1e-5, "L3_g1", "L3_be1"), 9: ("post", 1e-5, "L3_g2", "L3_be2"),
                10: ("post", 1e-5, "L3_g3", "L3_be3")}
        FEAT = ["xc_T", "cn_T", "h_T0", "a_T1", "a_T2", "h_T1", "a_T3", "h_T2", "a_T4", "a_T5", "h_T3"]
        FEAT_NORM = [None, 0, None, 3, 4, 5, 6, 7, None, None, None]
        NORM_FEAT = {1: 2, 3: 3, 4: 4, 5: 5, 6: 6, 7: 7, 8: 9, 9: 10}

        PROJECT_FEAT = [1, 4, 5, 7, 9, 10]
        UP_FEAT = [3, 6, 8, 11]
        PADT_UNITS = [1, 1, 1, 3, 4, 4]
        KT_UNITS = [1, 1, 1, 0, 4, 4]
        PADS_UNITS = [1, 1, 1, 3, 2, 2]
        ROT_PARTS = {SMALL: [(0, 256)], GQA: [(0, 512), (512, 512), (1024, 256)], WIDE: [(0, 512), (512, 512)]}
        ROT_UNITS = [0, 1, 1, 3, 2, 2]
        RAW_UNITS = [0, 0, 0, 4, 3, 3]
        AOT_UNITS = [1, 1, 1, 2, 1, 1]
        HID_UNITS = [4, 4, 1, 4]

        @block.tensor
        def _(pe):
            pe.wait_ge(weights_in, 16 * (len(vec_loads) + N_DIAG))
            pe.wait_ge(consts_set, 1)
            for c in range(NC):
                for name, n in PER_ITER.items():
                    pe.sem_inc(ev[c][name], n)
            now = Turn()
            order = [[], []]

            def take(c, name, streams=0):
                pe.wait_ge(last_reader(c, name), last_read_count(now.it, name))
                order[c].append(name)
                for _ in range(streams):
                    pe.matmul(bank(c, name)[:, :].rearrange("p (a n) -> p a n", a=4), ident_r[:, :],
                              ident_r[:, :].unsqueeze(1).broadcast_to([128, 4, 128]), start=True, stop=True,
                              skip_group_check=True)

            def transpose_into(c, name, pieces):
                for i, src in enumerate(pieces):
                    last = pe.transpose(bank(c, name)[0:src.shape[1], 128 * i:128 * i + 128], src, ident)
                last.then_inc(filled(c, name), 1)

            def product(c, name, pairs, at=0, last=True):
                n = pairs[0][1].shape[-1]
                for i, (lhsT, rhs) in enumerate(pairs):
                    mm = pe.matmul(bank(c, name)[:, at:at + n], lhsT, rhs,
                                   start=(i == 0), stop=(i == len(pairs) - 1))
                if last:
                    mm.then_inc(filled(c, name), 1)

            def to_features(c, f):
                t = cs[c]
                take(c, FEAT[f], STREAM["apply"][f - 1] if c == 0 else 0)
                pe.wait_ge(tok_ready[c], nth(now.it, "tok_ready", f))
                src = {1: t.cn, 3: t.xn, 4: t.xn, 5: t.xn, 6: t.xn, 7: t.xn}.get(f, t.x)
                transpose_into(c, FEAT[f], [src[:, :]])

            def project(c, a):
                t = cs[c]
                pe.wait_ge(feat_ready[c], nth(now.it, "feat_ready", PROJECT_FEAT[a]))
                hT = t.xcT[:, 0, :] if a == 0 else t.hT[:, :]
                cT = t.xcT[:, 1, :]
                if a in (0, 1, 2):
                    take(c, f"qkv{a}")
                    Wa = (W0, W1s, W1c)[a]
                    product(c, f"qkv{a}", [(hT, Wa[:, 0, :])], 0, False)
                    product(c, f"qkv{a}", [(hT if a == 1 else cT,
                                            Wa[:, 1:3, :].rearrange("p a n -> p (a n)"))], 128)
                elif a == 3:
                    for u in range(2):
                        take(c, f"q3_{u}")
                        product(c, f"q3_{u}", [(hT, W2q[:, 512 * u:512 * u + 512])])
                    take(c, "kv3")
                    product(c, "kv3", [(t.cnT[:, :], W2kv[:, :])])
                else:
                    for i, n in enumerate((f"q{a}_0", f"k{a}", f"v{a}")):
                        take(c, n)
                        if a == 4:
                            product(c, n, [(hT, W4[:, 512 * i:512 * i + 512])])
                        else:
                            product(c, n, [(cT if i else hT, W5[:, i, :])])

            def stack(c, a):
                t, kind = cs[c], ATT[a]["kind"]
                done = sum(PADS_UNITS[:a])
                take(c, f"qT{a}_0", STREAM["stack"][a] if c == 0 else 0)
                pe.wait_ge(pads_ready[c], nth(now.it, "pads_ready", done + 1))
                if kind == SMALL:
                    for nm, src in ((f"qT{a}_0", t.q8), (f"kT{a}_0", t.k8)):
                        flat = src[:, :, :, :].rearrange("p h s d -> p (h s d)")
                        if nm[0] == "k":
                            take(c, nm)
                        transpose_into(c, nm, [flat[:, 128 * i:128 * i + 128] for i in range(4)])
                elif kind == GQA:
                    for u in range(2):
                        if u:
                            take(c, "qT3_1")
                            pe.wait_ge(pads_ready[c], nth(now.it, "pads_ready", done + 2))
                        transpose_into(c, f"qT3_{u}",
                                       [t.raw[:, 512 * u + 128 * i:512 * u + 128 * i + 128] for i in range(4)])
                    take(c, "kT3_0")
                    pe.wait_ge(pads_ready[c], nth(now.it, "pads_ready", done + 3))
                    transpose_into(c, "kT3_0", [t.kdup[:, 128 * i:128 * i + 128] for i in range(4)])
                else:
                    for i, qk in enumerate("qk"):
                        if i:
                            pe.wait_ge(pads_ready[c], nth(now.it, "pads_ready", done + 2))
                        for j in range(4):
                            if i or j:
                                take(c, f"{qk}T{a}_{j}")
                            transpose_into(c, f"{qk}T{a}_{j}",
                                           [t.pads[:, i, 4 * j + p, :, :].rearrange("p s d -> p (s d)")
                                            for p in range(4)])

            def operands(c, a, j, p):
                t, kind = cs[c], ATT[a]["kind"]
                h = head_of(kind, j, p)
                if kind == SMALL:
                    rr = slice(32 * j, 32 * j + 32)
                    return t.qT[rr, 128 * p:128 * p + 128], t.kT[rr, 128 * p:128 * p + 128]
                if kind == GQA:
                    rr = slice(64 * (h % 2), 64 * (h % 2) + 64)
                    q = 128 * (h // 2)
                    kv = 128 * (h // 4)
                    return t.qT64[rr, q:q + 128], t.kT64[rr, kv:kv + 128]
                return t.qT[0:96, 128 * h:128 * h + 128], t.kT[0:96, 128 * h:128 * h + 128]

            def biases(c, a):
                if ATT[a]["bias"] == "causal":
                    return [causal_r[:, :]]
                if ATT[a]["bias"] == "mask":
                    return [cs[c].mask_hi[:, :], cs[c].mask_lo[:, :]]
                return []

            def scores(c, a, j):
                nk = ATT[a]["nk"]
                nke = S if nk == S else SKE
                if j == 0:
                    pe.wait_ge(padT_ready[c], nth(now.it, "padT_ready", sum(PADT_UNITS[:a + 1])))
                    if KT_UNITS[a]:
                        pe.wait_ge(kT_ready[c], nth(now.it, "kT_ready", sum(KT_UNITS[:a + 1])))
                name = f"s{a}_{j}"
                take(c, name)
                dst = bank(c, name)[:, 0:4 * nke]
                bs = biases(c, a)
                for i, bias in enumerate(bs):
                    pe.matmul(dst.rearrange("q (h k) -> q h k", h=4), ident_r[:, :],
                              bias.unsqueeze(1).broadcast_to([128, 4, nke]),
                              start=(i == 0), stop=False, skip_group_check=True)
                for p in range(4):
                    qT, kT = operands(c, a, j, p)
                    mm = pe.matmul(dst[:, nke * p:nke * p + nke], qT, kT[:, 0:nke],
                                   start=not bs, stop=True, skip_group_check=True)
                mm.then_inc(filled(c, name), 1)

            def maxima(c, a):
                take(c, f"nm{a}", STREAM["max"][a])
                pe.wait_ge(nm_ready[c], nth(now.it, "nm_ready", a + 1))
                transpose_into(c, f"nm{a}", [cs[c].nm[:, :]])

            def scores_T(c, a, j):
                t, nk, kind = cs[c], ATT[a]["nk"], ATT[a]["kind"]
                if j == 0:
                    pe.wait_ge(nmT_ready[c], nth(now.it, "nmT_ready", a + 1))
                name = f"sT{a}_{j}"
                take(c, name)
                dst = bank(c, name)[0:nk, :]
                heads = dst.rearrange("k (h q) -> k h q", h=4)
                at = 4 * KINDS.index(kind) + j
                pe.matmul(heads, sel_r[:, at:at + 1].broadcast_to([128, nk]), t.nmT[:, :, :],
                          start=True, stop=False, skip_group_check=True)
                for bias in biases(c, a):
                    pe.matmul(heads, bias[:, 0:nk], ident_r[:, :].unsqueeze(1).broadcast_to([128, 4, S]),
                              start=False, stop=False, skip_group_check=True)
                for p in range(4):
                    qT, kT = operands(c, a, j, p)
                    mm = pe.matmul(dst[:, 128 * p:128 * p + 128], kT[:, 0:nk], qT,
                                   start=False, stop=True, skip_group_check=True)
                mm.then_inc(filled(c, name), 1)

            def values(c, a, quarter):
                t, kind, hd = cs[c], ATT[a]["kind"], ATT[a]["hd"]
                v = v_tile(c, a)
                where = {head_of(kind, j, p): 4 * j + p for j in range(4) for p in range(4)}
                per = NH // PV_UNITS[kind]
                if quarter == 0:
                    take(c, f"pv{a}_0")
                    pe.wait_ge(probs_ready[c], nth(now.it, "probs_ready", 4 * a + 4))
                for h in range(4 * quarter, 4 * quarter + 4):
                    u, i = h // per, h % per
                    name = f"pv{a}_{u}"
                    if i == 0 and h:
                        take(c, name)
                    at = 128 * where[h]
                    vh = (hd + 1) * (h // 4 if kind == GQA else h)
                    mm = pe.matmul(bank(c, name)[:, (hd + 1) * i:(hd + 1) * i + PV_N],
                                   t.probs[:, at:at + 128], v[:, vh:vh + PV_N],
                                   start=True, stop=True, skip_group_check=True)
                    if i == per - 1:
                        mm.then_inc(filled(c, name), 1)

            def out_T(c, a):
                n = NH * ATT[a]["hd"] // 128
                last = f"pv{a}_{PV_UNITS[ATT[a]['kind']] - 1}"
                for u in range(AOT_UNITS[a]):
                    take(c, f"oT{a}_{u}")
                    if u == 0:
                        pe.wait_ge(reader(c, last), read_count(now.it, last))
                    transpose_into(c, f"oT{a}_{u}", [cs[c].ao[:, 128 * i:128 * i + 128]
                                                     for i in range(4 * u, min(n, 4 * u + 4))])

            def out_product(c, a):
                n = NH * ATT[a]["hd"] // 128
                pe.wait_ge(aoT_ready[c], nth(now.it, "aoT_ready", sum(AOT_UNITS[:a + 1])))
                take(c, f"y{a}")
                product(c, f"y{a}", [(cs[c].aoT[:, 128 * i:128 * i + 128], Wo[a][:, i, :]) for i in range(n)])

            def up(c, n):
                pe.wait_ge(feat_ready[c], nth(now.it, "feat_ready", UP_FEAT[n]))
                for nm, W in ((f"up{n}", Wup[n]),) if n != 2 else (("gate2", Wgate), ("up2", Wup[2])):
                    take(c, nm)
                    for m in range(4):
                        product(c, nm, [(W[:, 128 * m:128 * m + 128], cs[c].hT[:, :])], 128 * m, m == 3)

            def down(c, n):
                take(c, f"down{n}", STREAM["down"][n] if c == 0 else 0)
                if n == 2:
                    pe.wait_ge(hidden2_ready[c], nth(now.it, "hidden2_ready", 1))
                else:
                    pe.wait_ge(act_hidden[c], nth(now.it, "act_hidden", sum(HID_UNITS[:n + 1])))
                product(c, f"down{n}", [(cs[c].hid[:, 128 * m:128 * m + 128], Wdown[n][:, m, :])
                                        for m in range(4)])

            def run(st, c):
                if st[0] == "inputs":
                    take(c, "xc_T", STREAM["inputs"] if c == 0 else 0)
                    pe.wait_ge(loaded[c], now.it * (16 * N_LOADS) + 16 * N_LOADS)
                    transpose_into(c, "xc_T", [cs[c].x_in[:, :], cs[c].c_in[:, :]])
                elif st[0] == "contextT":
                    to_features(c, 1)
                elif st[0] == "project":
                    project(c, st[1])
                elif st[0] == "stack":
                    stack(c, st[1])
                elif st[0] == "scores":
                    scores(c, st[1], st[2])
                elif st[0] == "max":
                    maxima(c, st[1])
                elif st[0] == "probs":
                    scores_T(c, st[1], st[2])
                elif st[0] == "values":
                    values(c, st[1], st[2])
                elif st[0] == "outT":
                    out_T(c, st[1])
                elif st[0] == "out":
                    out_product(c, st[1])
                elif st[0] == "apply" and st[1] in NORM_FEAT:
                    to_features(c, NORM_FEAT[st[1]])
                elif st[0] == "copyT":
                    to_features(c, 8)
                elif st[0] == "up":
                    up(c, st[1])
                elif st[0] == "down":
                    down(c, st[1])
            in_turn(pe, now, run)
            assert order == [NAMES, NAMES]

        @block.scalar
        def _(act):
            act.wait_ge(weights_in, 16 * (len(vec_loads) + N_DIAG))
            now = Turn()

            def evacuate(c, name, dst, width, event, scale=None, bias=None, n=128):
                act.wait_ge(filled(c, name), filled_count(now.it, name))
                act.activation(dst, bank(c, name)[0:n, 0:width], ACT.Identity,
                               scale=1.0 if scale is None else scale,
                               bias=0.0 if bias is None else bias).then_inc(event[c], 1)

            def to_features(c, f):
                t = cs[c]
                dst = t.xcT[:, :, :].rearrange("p a n -> p (a n)") if f == 0 else t.cnT[:, :] if f == 1 else t.hT[:, :]
                g = b = None
                if FEAT_NORM[f] is not None:
                    _, _, gain, shift = NORM[FEAT_NORM[f]]
                    g, b = col(gain), col(shift) if shift else None
                evacuate(c, FEAT[f], dst, 256 if f == 0 else 128, feat_ready, g, b)

            def project(c, a):
                t = cs[c]
                if a == 3:
                    for u in range(2):
                        evacuate(c, f"q3_{u}", t.raw[:, 512 * u:512 * u + 512], 512, raw_ready)
                    act.wait_ge(filled(c, "kv3"), filled_count(now.it, "kv3"))
                    act.activation(t.raw[:, 1024:1280], bank(c, "kv3")[:, 0:256],
                                   ACT.Identity).then_inc(raw_ready[c], 1)
                    act.activation(v_heads(c, a)[:, :, 0:64],
                                   bank(c, "kv3")[0:SK, 256:512].rearrange("p (h d) -> p h d", h=4),
                                   ACT.Identity).then_inc(raw_ready[c], 1)
                elif a > 3:
                    evacuate(c, f"q{a}_0", t.raw[:, 0:512], 512, raw_ready)
                    evacuate(c, f"k{a}", t.raw[:, 512:1024], 512, raw_ready)
                    act.wait_ge(filled(c, f"v{a}"), filled_count(now.it, f"v{a}"))
                    nk = ATT[a]["nk"]
                    act.activation(v_heads(c, a)[:, :, 0:32],
                                   bank(c, f"v{a}")[0:nk, :].rearrange("p (h d) -> p h d", h=NH),
                                   ACT.Identity).then_inc(raw_ready[c], 1)

            def stack(c, a):
                t, kind = cs[c], ATT[a]["kind"]
                if kind == SMALL:
                    evacuate(c, f"qT{a}_0", t.qT[:, 0:512], 512, padT_ready)
                elif kind == GQA:
                    for u in range(2):
                        evacuate(c, f"qT3_{u}", t.qT64[:, 512 * u:512 * u + 512], 512, padT_ready)
                    evacuate(c, "kT3_0", t.kT64[:, :], 512, padT_ready)
                else:
                    for j in range(4):
                        evacuate(c, f"qT{a}_{j}", t.qT[0:96, 512 * j:512 * j + 512], 512, padT_ready, n=96)

            def turn(c, a):
                if ATT[a]["kind"] != WIDE:
                    return
                t, done = cs[c], 2 * (a - 4)
                for i, dst in enumerate((t.pads[:, 0, :, 0:2, :], t.pads[:, 1, :, 0:3:2, :])):
                    act.wait_ge(roped[c], nth(now.it, "roped", done + i + 1))
                    src = t.raw[:, 512 * i:512 * i + 512].rearrange("p (h d) -> p h d", h=NH)
                    act.activation(dst.bitcast(F32R), src.unsqueeze(2).broadcast_to([128, NH, 2, 32]),
                                   ACT.Identity).then_inc(hi_ready[c], 1)

            def probs(c, a, j):
                t, nk, name = cs[c], ATT[a]["nk"], f"sT{a}_{j}"
                act.wait_ge(filled(c, name), filled_count(now.it, name))
                act.activation(t.probs[0:nk, 512 * j:512 * j + 512], bank(c, name)[0:nk, :], ACT.Exp,
                               scale=ATT[a]["scale"]).then_inc(probs_ready[c], 1)

            def up(c, n):
                t = cs[c]
                if n == 2:
                    act.wait_ge(filled(c, "gate2"), filled_count(now.it, "gate2"))
                    act.activation(t.gate, bank(c, "gate2")[:, :], ACT.Silu).then_inc(act_hidden[c], 1)
                    return
                act.wait_ge(filled(c, f"up{n}"), filled_count(now.it, f"up{n}"))
                for m in range(4):
                    act.activation(t.hid[:, 128 * m:128 * m + 128], bank(c, f"up{n}")[:, 128 * m:128 * m + 128],
                                   ACT.Relu if n == 0 else ACT.Gelu_apprx_tanh,
                                   bias=mlp_bias[:, n, m:m + 1]).then_inc(act_hidden[c], 1)

            def run(st, c):
                if st[0] == "inputs":
                    to_features(c, 0)
                elif st[0] == "contextT":
                    to_features(c, 1)
                elif st[0] == "project":
                    project(c, st[1])
                elif st[0] == "turn":
                    turn(c, st[1])
                elif st[0] == "stack":
                    stack(c, st[1])
                elif st[0] == "probs":
                    probs(c, st[1], st[2])
                elif st[0] == "outT":
                    a = st[1]
                    n = NH * ATT[a]["hd"] // 128
                    for u in range(AOT_UNITS[a]):
                        width = 128 * (min(n, 4 * u + 4) - 4 * u)
                        evacuate(c, f"oT{a}_{u}", cs[c].aoT[:, 512 * u:512 * u + width], width, aoT_ready)
                elif st[0] == "apply" and st[1] in NORM_FEAT:
                    to_features(c, NORM_FEAT[st[1]])
                elif st[0] == "copyT":
                    to_features(c, 8)
                elif st[0] == "up":
                    up(c, st[1])

            in_turn(act, now, run)

        @block.gpsimd
        def _(pool):
            pool.memset(W0[:, :, :], 0.0).then_inc(zeroed, 1)
            for c in range(NC):
                pool.memset(cs[c].c_in[:, :], 0.0).then_inc(zeroed, 1)
            pool.memset(minus_half[:, :], -0.5).then_inc(pool_step, 1)
            pool.wait_ge(pool_step, 1)
            pool.wait_ge(weights_in, 16 * (len(vec_loads) + N_DIAG))
            now = Turn()

            def inverse_std(c, n):
                pool.wait_ge(stats_ready[c], nth(now.it, "stats_ready", n + 1))
                pool.tensor_tensor(cs[c].rstd[:, :], cs[c].var[:, :], minus_half[:, :],
                                   ALU.pow).then_inc(rstd_ready[c], 1)

            def turned(c, a):
                t, hd, kind = cs[c], ATT[a]["hd"], ATT[a]["kind"]
                order = "p (h f t) -> p t h f" if kind == WIDE else "p (h t f) -> p t h f"
                half = "p (f t) -> p t f" if kind == WIDE else "p (t f) -> p t f"
                sin = table(f"sin{hd}").rearrange(half, t=2)
                for i, (at, width) in enumerate(ROT_PARTS[kind]):
                    if kind == SMALL:
                        pool.wait_ge(raw8_ready[c], nth(now.it, "raw8_ready", a))
                    else:
                        pool.wait_ge(raw_ready[c], nth(now.it, "raw_ready", sum(RAW_UNITS[:a]) + i + 1))
                    n = width // hd
                    src = t.raw[:, at:at + width].rearrange(order, h=n, t=2)
                    dst = t.turn[kind][:, at:at + width].rearrange(order, h=n, t=2)
                    for x in range(2):
                        ins_ = pool.tensor_tensor(dst[:, x], src[:, 1 - x],
                                                  sin[:, x].unsqueeze(1).broadcast_to([128, n, hd // 2]), ALU.mult)
                    ins_.then_inc(rot_ready[c], 1)

            def run(st, c):
                if st[0] == "stats":
                    inverse_std(c, st[1])
                elif st[0] == "project" and st[1] > 0:
                    turned(c, st[1])

            in_turn(pool, now, run)

        @block.vector
        def _(dve):
            dve.wait_ge(weights_in, 16 * (len(vec_loads) + N_DIAG))
            for c in range(NC):
                t = cs[c]
                dve.memset(t.q8[:, :, 3, :], 0.0).then_inc(dve_step, 1)
                dve.memset(t.k8[:, :, 3, :], 0.0).then_inc(dve_step, 1)
                dve.memset(t.mask8[:, :], 0.0).then_inc(dve_step, 1)
                dve.memset(t.nm[:, :], 0.0).then_inc(dve_step, 1)
                dve.memset(t.pads[:, :, :, :, :], 0.0).then_inc(dve_step, 1)
                for a in V_OF:
                    dve.memset(v_tile(c, a)[:, :], 0.0).then_inc(dve_step, 1)
            CLEARED = NC * (5 + len(V_OF))
            dve.wait_ge(dve_step, CLEARED)
            for c in range(NC):
                dve.memset(cs[c].q8[:, :, 3, 0:1], 1.0).then_inc(dve_step, 1)
                for a in V_OF:
                    hd = ATT[a]["hd"]
                    dve.memset(v_heads(c, a)[:, :, hd:hd + 1], 1.0).then_inc(dve_step, 1)
            dve.tensor_copy(ident_r[:, :], ident).then_inc(dve_step, 1)
            dve.tensor_copy(causal_r[:, :], table("causal")).then_inc(dve_step, 1)
            dve.tensor_copy(sel_r[:, :], table("selector")[:, 0:12]).then_inc(dve_step, 1)
            ONCE = CLEARED + NC * (1 + len(V_OF)) + 3
            dve.wait_ge(dve_step, ONCE)
            dve.sem_inc(consts_set, 1)

            now = Turn()

            def step(ins):
                ins.then_inc(dve_step, 1)
                now.steps += 1

            def settle(apart=False):
                dve.wait_ge(dve_step, now.it * DVE_STEPS + (ONCE + now.steps))
                if apart:
                    dve.memset(wait_carrier[:, :], 0.0)

            def link(ins, apart=False):
                step(ins)
                settle(apart)

            def statistics(c, n, src):
                t = cs[c]
                kind, eps, _, _ = NORM[n]
                link(dve.bn_stats(t.stats[:, :], src), apart=True)
                link(dve.bn_aggr(t.mv[:, :], t.stats[:, :]))
                if kind == "rms":
                    link(dve.scalar_tensor_tensor(t.var[:, :], t.mv[:, 0:1], t.mv[:, 0:1], t.mv[:, 1:2],
                                                  ALU.mult, ALU.add))
                    dve.tensor_scalar(t.var[:, :], t.var[:, :], eps, None,
                                      ALU.add).then_inc(stats_ready[c], 1)
                else:
                    dve.tensor_scalar(t.var[:, :], t.mv[:, 1:2], eps, None,
                                      ALU.add).then_inc(stats_ready[c], 1)

            def apply(c, n):
                t = cs[c]
                kind, _, g, b = NORM[n]
                dve.wait_ge(rstd_ready[c], nth(now.it, "rstd_ready", n + 1))
                if kind == "rms":
                    src, dst = (t.c_in, t.cn) if n == 0 else (t.x, t.xn)
                    dve.tensor_scalar(dst[:, :], src[:, :], t.rstd[:, :], None,
                                      ALU.mult).then_inc(tok_ready[c], 1)
                elif kind == "pre":
                    dve.tensor_scalar(t.xn[:, :], t.x[:, :], t.mv[:, 0:1], t.rstd[:, :],
                                      ALU.subtract, ALU.mult).then_inc(tok_ready[c], 1)
                else:
                    link(dve.tensor_scalar(t.xn[:, :], t.x[:, :], t.mv[:, 0:1], t.rstd[:, :],
                                           ALU.subtract, ALU.mult))
                    link(dve.tensor_tensor(t.xn[:, :], t.xn[:, :], row(g), ALU.mult))
                    if n == 10:
                        dve.wait_ge(stored[c], now.it * 16 + 16)
                        dve.tensor_tensor(t.y[:, :], t.xn[:, :], row(b),
                                          ALU.add).then_inc(out_ready[c], 1)
                    else:
                        ins_ = dve.tensor_tensor(t.x[:, :], t.xn[:, :], row(b), ALU.add)
                        if n == 2:
                            link(ins_)
                        else:
                            ins_.then_inc(tok_ready[c], 1)

            def add_to_x(c, name, bias, first=False):
                t = cs[c]
                dve.wait_ge(filled(c, name), filled_count(now.it, name))
                ins_ = dve.tensor_tensor(t.x[:, :], bank(c, name)[:, 0:128],
                                         t.x_in[:, :] if first else t.x[:, :], ALU.add)
                ins_.then_inc(added[c], 1)
                dve.wait_ge(reader(c, name), read_count(now.it, name))
                if bias:
                    ins_ = dve.tensor_tensor(t.x[:, :], t.x[:, :], row(bias), ALU.add)
                    if first:
                        ins_.then_inc(inputs_used[c], 1)
                        dve.wait_ge(inputs_used[c], nth(now.it, "inputs_used", 1))
                    else:
                        link(ins_)

            def inputs(c):
                t = cs[c]
                dve.wait_ge(loaded[c], now.it * (16 * N_LOADS) + 16 * N_LOADS)
                link(dve.tensor_scalar(t.zero[0:SK, :], t.key_mask[0:SK, :], 0.0, None, ALU.is_equal))
                step(dve.tensor_scalar(t.keep[0:SK, :], t.zero[0:SK, :], -1.0, 1.0, ALU.mult, ALU.add))
                step(dve.tensor_scalar(t.kbias[0:SK, :], t.zero[0:SK, :], -1e20, None, ALU.mult))
                settle()

            def mask(c):
                t = cs[c]
                link(dve.tensor_scalar(t.mask8[:, 0:SK], t.mask_in[:, :], 8.0, -3e38, ALU.mult, ALU.max))
                link(dve.tensor_copy(t.mask_hi[:, :], t.mask8[:, :]))
                step(dve.tensor_tensor(t.mask_lo[:, :], t.mask8[:, :], t.mask_hi[:, :].bitcast(F32), ALU.subtract))

            def project(c, a):
                t = cs[c]
                if ATT[a]["kind"] != SMALL:
                    return
                name = f"qkv{a}"
                dve.wait_ge(filled(c, name), filled_count(now.it, name))
                src = bank(c, name)
                if a == 0:
                    step(dve.tensor_copy(t.raw[:, 0:256], src[:, 0:256]))
                    dve.tensor_copy(v_heads(c, a)[:, :, 0:8],
                                    src[0:SK, 256:384].rearrange("p (h d) -> p h d", h=NH)).then_inc(qkv_read[c], 1)
                    dve.wait_ge(reader(c, name), read_count(now.it, name))
                    link(dve.tensor_scalar(t.raw[0:SK, 128:256], t.raw[0:SK, 128:256], t.keep[0:SK, :], None,
                                           ALU.mult))
                    return
                i = ROWS.index("L1_sa_bq" if a == 1 else "L1_ca_bq")
                dve.tensor_tensor(t.raw[:, 0:256], src[:, 0:256],
                                  rows[:, i:i + 2, :].rearrange("p a n -> p (a n)"),
                                  ALU.add).then_inc(raw8_ready[c], 1)
                nk = ATT[a]["nk"]
                dve.tensor_tensor(v_heads(c, a)[:, :, 0:8],
                                  src[0:nk, 256:384].rearrange("p (h d) -> p h d", h=NH),
                                  rows[0:nk, i + 2, :].rearrange("p (h d) -> p h d", h=NH),
                                  ALU.add).then_inc(qkv_read[c], 1)
                dve.wait_ge(raw8_ready[c], nth(now.it, "raw8_ready", a))

            def turn(c, a):
                t, hd, kind = cs[c], ATT[a]["hd"], ATT[a]["kind"]
                if a == 0:
                    return
                for i, (at, width) in enumerate(ROT_PARTS[kind]):
                    if kind != SMALL:
                        dve.wait_ge(raw_ready[c], nth(now.it, "raw_ready", sum(RAW_UNITS[:a]) + i + 1))
                    n = width // hd
                    step(dve.tensor_tensor(t.cosd[:, at:at + width].rearrange("p (h d) -> p h d", h=n),
                                           t.raw[:, at:at + width].rearrange("p (h d) -> p h d", h=n),
                                           table(f"cos{hd}").unsqueeze(1).broadcast_to([128, n, hd]), ALU.mult))
                settle()
                for i, (at, width) in enumerate(ROT_PARTS[kind]):
                    dve.wait_ge(rot_ready[c], nth(now.it, "rot_ready", sum(ROT_UNITS[:a]) + i + 1))
                    ins_ = dve.tensor_tensor(t.raw[:, at:at + width], t.cosd[:, at:at + width],
                                             t.turn[kind][:, at:at + width], ALU.add)
                    if kind == WIDE:
                        ins_.then_inc(roped[c], 1)
                    elif kind == SMALL or i == 2:
                        link(ins_)
                    else:
                        ins_.then_inc(pads_ready[c], 1)

            def stack(c, a):
                t, kind = cs[c], ATT[a]["kind"]
                if kind == GQA:
                    k = t.raw[:, 1024:1280].rearrange("p (h d) -> p h d", h=4)
                    dup = t.kdup.rearrange("p (h r d) -> p h r d", h=4, r=2)
                    dve.tensor_copy(dup, k.unsqueeze(2).broadcast_to([128, 4, 2, 64])
                                    ).then_inc(pads_ready[c], 1)
                    return
                hd = ATT[a]["hd"]
                n = NH * hd
                q = t.raw[:, 0:n].rearrange("p (h d) -> p h d", h=NH)
                k = t.raw[:, n:2 * n].rearrange("p (h d) -> p h d", h=NH)
                if kind == WIDE:
                    done = 2 * (a - 4)
                    dve.wait_ge(hi_ready[c], nth(now.it, "hi_ready", done + 1))
                    dve.tensor_tensor(t.pads[:, 0, :, 2, :], q, t.pads[:, 0, :, 0, :],
                                      ALU.subtract).then_inc(pads_ready[c], 1)
                    dve.wait_ge(hi_ready[c], nth(now.it, "hi_ready", done + 2))
                    dve.tensor_tensor(t.pads[:, 1, :, 1, :], k, t.pads[:, 1, :, 0, :],
                                      ALU.subtract).then_inc(pads_ready[c], 1)
                    return
                if a == 0:
                    step(dve.tensor_copy(t.k8[0:SK, :, 3, 0:1],
                                         t.kbias[0:SK, :].unsqueeze(1).broadcast_to([SK, NH, 1])))
                elif a == 1:
                    step(dve.memset(t.k8[:, :, 3, 0:1], 0.0))
                step(dve.tensor_copy(t.q8[:, :, 0:2, :].bitcast(F32R), q.unsqueeze(2).broadcast_to([128, NH, 2, hd])))
                link(dve.tensor_copy(t.k8[:, :, 0:3:2, :].bitcast(F32R),
                                     k.unsqueeze(2).broadcast_to([128, NH, 2, hd])))
                step(dve.tensor_tensor(t.q8[:, :, 2, :], q, t.q8[:, :, 0, :], ALU.subtract))
                dve.tensor_tensor(t.k8[:, :, 1, :], k, t.k8[:, :, 0, :],
                                  ALU.subtract).then_inc(pads_ready[c], 1)

            def stack_k(c, a):
                n = 128 if ATT[a]["kind"] == SMALL else 96
                for j in range(KT_UNITS[a]):
                    name = f"kT{a}_{j}"
                    dve.wait_ge(filled(c, name), filled_count(now.it, name))
                    dve.tensor_copy(cs[c].kT[0:n, 512 * j:512 * j + 512],
                                    bank(c, name)[0:n, :]).then_inc(kT_ready[c], 1)

            def scores(c, a, j):
                t, nk, name = cs[c], ATT[a]["nk"], f"s{a}_{j}"
                nke = S if nk == S else SKE
                dve.wait_ge(filled(c, name), filled_count(now.it, name))
                src = bank(c, name)[:, 0:4 * nke].rearrange("p (h k) -> p h k", h=4)[:, :, 0:nk]
                dve.tensor_reduce(t.nmax[:, 4 * j:4 * j + 4], src, AX.X, ALU.max,
                                  negate=True).then_inc(score_read[c], 1)

            def halves(c, a):
                t = cs[c]
                dve.wait_ge(reader(c, f"s{a}_3"), read_count(now.it, f"s{a}_3"))
                link(dve.tensor_copy(t.nm[:, 0:NH].bitcast(F32R), t.nmax[:, :]))
                dve.tensor_tensor(t.nm[:, NH:2 * NH], t.nmax[:, :], t.nm[:, 0:NH],
                                  ALU.subtract).then_inc(nm_ready[c], 1)
                name, at = f"nm{a}", 12 + 4 * KINDS.index(ATT[a]["kind"])
                dve.wait_ge(filled(c, name), filled_count(now.it, name))
                dve.tensor_tensor(t.nmT[:, :, :], bank(c, name)[:, 0:S].unsqueeze(1).broadcast_to([128, 4, S]),
                                  table("selector")[:, at:at + 4].unsqueeze(2).broadcast_to([128, 4, S]),
                                  ALU.mult).then_inc(nmT_ready[c], 1)

            def values(c, a, quarter):
                t, kind, hd = cs[c], ATT[a]["kind"], ATT[a]["hd"]
                per = NH // PV_UNITS[kind]
                if (4 * quarter + 4) % per:
                    return
                u = 4 * quarter // per
                name = f"pv{a}_{u}"
                dve.wait_ge(filled(c, name), filled_count(now.it, name))
                src = bank(c, name)[:, 0:per * (hd + 1)].rearrange("p (h d) -> p h d", h=per)
                rs = t.rsum[:, u * per:(u + 1) * per].unsqueeze(2)
                link(dve.reciprocal(rs, src[:, :, hd:hd + 1]))
                dst = t.ao[:, u * per * hd:(u + 1) * per * hd].rearrange("p (h d) -> p h d", h=per)
                dve.tensor_tensor(dst, src[:, :, 0:hd], rs.broadcast_to([128, per, hd]),
                                  ALU.mult).then_inc(ao_ready[c], 1)

            def up2(c):
                t = cs[c]
                dve.wait_ge(act_hidden[c], nth(now.it, "act_hidden", sum(HID_UNITS[:3])))
                dve.wait_ge(filled(c, "up2"), filled_count(now.it, "up2"))
                dve.tensor_tensor(t.hid, bank(c, "up2")[:, :], t.gate,
                                  ALU.mult).then_inc(hidden2_ready[c], 1)

            OUT_BIAS = ["L0_b_out", "L1_sa_bo", "L1_ca_bo", None, None, None]
            DOWN_BIAS = ["L0_b_ff2", "L1_fc2_b", None, "L3_b_ff2"]
            def run(st, c):
                if st[0] == "inputs":
                    inputs(c)
                elif st[0] == "project":
                    project(c, st[1])
                elif st[0] == "turn":
                    turn(c, st[1])
                elif st[0] == "stack":
                    stack(c, st[1])
                elif st[0] == "stack_k":
                    stack_k(c, st[1])
                elif st[0] == "scores":
                    scores(c, st[1], st[2])
                elif st[0] == "max":
                    halves(c, st[1])
                elif st[0] == "values":
                    values(c, st[1], st[2])
                elif st[0] == "out":
                    add_to_x(c, f"y{st[1]}", OUT_BIAS[st[1]], first=st[1] == 0)
                elif st[0] == "stats":
                    statistics(c, st[1], (cs[c].x if st[1] else cs[c].c_in)[:, :])
                elif st[0] == "mask":
                    mask(c)
                elif st[0] == "apply":
                    apply(c, st[1])
                elif st == ("up", 2):
                    up2(c)
                elif st[0] == "down":
                    add_to_x(c, f"down{st[1]}", DOWN_BIAS[st[1]])
                elif st[0] == "copyT":
                    dve.sem_inc(tok_ready[c], 1)
            in_turn(dve, now, run)
            assert now.steps == DVE_STEPS, ("DVE_STEPS", now.steps)



def host_constants():
    import numpy as np

    at = np.arange(S)
    c = {"ident": np.eye(S), "causal": np.where(at[None, :] <= at[:, None], 0.0, -2.0 ** 100)}
    select = np.zeros((128, 2, 3, 4))
    for i, kind in enumerate(KINDS):
        for j in range(4):
            for p in range(4):
                for r in (head_of(kind, j, p), 16 + head_of(kind, j, p)):
                    select[r, 0, i, j] = select[r, 1, i, p] = 1.0
    c["selector"] = select.reshape(128, 24)
    for hd, pairs in ((8, False), (64, False), (32, True)):
        inv = (np.float32(1.0) / np.power(np.float32(10000.0), np.arange(0, hd, 2, dtype=np.float32) / np.float32(hd)))
        f = at.astype(np.float32)[:, None] * inv.astype(np.float32)[None, :]
        cos, sin = np.cos(f), np.sin(f)
        if pairs:
            c[f"cos{hd}"] = np.repeat(cos, 2, axis=1)
            c[f"sin{hd}"] = np.stack([-sin, sin], axis=-1).reshape(S, hd)
        else:
            c[f"cos{hd}"] = np.concatenate([cos, cos], axis=1)
            c[f"sin{hd}"] = np.concatenate([-sin, sin], axis=1)
    return np.ascontiguousarray(np.concatenate([c[n] for n in HOST], axis=1).astype(np.float32))


def kernel(**inputs):
    import numpy as np
    import concourse.bacc as bacc
    from concourse.bass_utils import run_bass_kernel_spmd

    nc = bacc.Bacc("TRN2", target_bir_lowering=False, num_devices=1)
    arrays, aps = {}, {}
    for name, value in inputs.items():
        a = np.ascontiguousarray(value)
        arrays[f"in_{name}"] = a
        aps[name] = nc.dram_tensor(f"in_{name}", a.shape, mybir.dt.from_np(a.dtype), kind="ExternalInput").ap()
    k = host_constants()
    arrays["constants"] = k
    kap = nc.dram_tensor("constants", k.shape, F32, kind="ExternalInput").ap()
    out = nc.dram_tensor("out", (B, S, E), F32, kind="ExternalOutput").ap()
    build(nc, aps, kap, out)
    r = run_bass_kernel_spmd(nc, [arrays], core_ids=[0])
    return r.results[0]["out"]
```
